# Optimizing a Trainium2 kernel written in Bass

```python
import numpy as np
import jax
import jax.numpy as jnp

def _softmax(x, axis=-1):
    return jax.nn.softmax(x, axis=axis)

def _gelu(x):
    return jax.nn.gelu(x, approximate=True)

def _silu(x):
    return jax.nn.silu(x)

def _sigmoid(x):
    return jax.nn.sigmoid(x)

def _layernorm(x, axis=-1, eps=1e-05):
    m = jnp.mean(x, axis=axis, keepdims=True)
    v = jnp.var(x, axis=axis, keepdims=True)
    return (x - m) / jnp.sqrt(v + eps)

def _scatter_add(tgt, idx, src, axis=0):
    return tgt.at[idx].add(src)

def _segment_sum(src, seg, n):
    return jax.ops.segment_sum(src, seg, n)
kernel_name = 'mk_decoder_preln_d1_seqx_r8_babda7'

def setup_inputs(seed: int=0):
    np.random.seed(seed)
    _w = jnp.asarray

    def _rec_inputs():
        import jax
        import jax.numpy as jnp
        _rk = jax.random.key(seed)
        x = -0.0002928 + 1 * jax.random.normal(jax.random.fold_in(_rk, 1), (16, 128, 128), jnp.float32)
        _lenS = 128 - jax.random.randint(jax.random.fold_in(_rk, 7), (16,), 0, max(1, 128 // 4) + 1, jnp.int32)
        _lenS2 = 128 - jax.random.randint(jax.random.fold_in(_rk, 8), (16,), 0, max(1, 128 // 4) + 1, jnp.int32)
        _ctx_1024P = jax.random.normal(jax.random.fold_in(_rk, 11), (16, 16, 128), jnp.float32)
        _ctx_1024c = jax.random.dirichlet(jax.random.fold_in(_rk, 511), 0.3 * jnp.ones((16,), jnp.float32), (16, 128))
        _ctx_1024t = jnp.einsum('bsk,bkd->bsd', _ctx_1024c, _ctx_1024P)
        _ctx_1024t = _ctx_1024t * jax.lax.rsqrt(jnp.mean(jnp.square(_ctx_1024t)) + 1e-12) * 0.953939
        ctx_1024 = -1.39393e-06 + 0.999914 * (_ctx_1024t + 0.3 * jax.random.normal(jax.random.fold_in(_rk, 611), (16, 128, 128), jnp.float32))
        return (x, ctx_1024)
    x, ctx_1024 = _rec_inputs()

    def _L0_attn_setup():
        import jax, jax.numpy as jnp
        import numpy as np
        NUM_HEADS = 16

        def _rope_tables(seq_len, head_dim, dtype):
            pos = jnp.arange(seq_len, dtype=jnp.float32)
            inv = jnp.power(10000.0, -2.0 * jnp.arange(head_dim // 2, dtype=jnp.float32) / head_dim)
            ang = pos[:, None] * inv[None, :]
            cos = jnp.repeat(jnp.cos(ang), 2, axis=-1).astype(dtype)
            sin = jnp.repeat(jnp.sin(ang), 2, axis=-1).astype(dtype)
            return (cos[None, None], sin[None, None])

        def _rotate_half_interleaved(x):
            x2 = jnp.stack([-x[..., 1::2], x[..., ::2]], axis=-1)
            return x2.reshape(x.shape)
        key = jax.random.key(seed)
        k0, k1, k2, k3 = jax.random.split(key, 4)
        B, N, C = (2, 256, 128)
        s = 1.0 / np.sqrt(C)
        return {'x': jax.random.normal(k0, (B, N, C), dtype=jnp.float32), 'Wq': jax.random.normal(k1, (C, C), dtype=jnp.float32) * s, 'Wk': jax.random.normal(k2, (C, C), dtype=jnp.float32) * s, 'Wv': jax.random.normal(k3, (C, C), dtype=jnp.float32) * s}
    _L0_attn_all = _L0_attn_setup()
    _L0_attn_in = {k: v for k, v in _L0_attn_all.items() if k in ('Wq', 'Wk', 'Wv')}
    del _L0_attn_all

    def _L0_xattn_setup():
        import jax, jax.numpy as jnp
        import numpy as np
        D_MODEL = 128
        NUM_HEADS = 16
        HEAD_DIM = D_MODEL // NUM_HEADS
        key = jax.random.key(seed)
        ks = jax.random.split(key, 11)
        B, S, D = (2, 256, D_MODEL)
        s = 1.0 / np.sqrt(D)
        inp = {'query': jax.random.normal(ks[0], (B, S, D), jnp.float32), 'key': jax.random.normal(ks[1], (B, S, D), jnp.float32), 'value': jax.random.normal(ks[2], (B, S, D), jnp.float32), 'Wq': jax.random.normal(ks[3], (D, D), jnp.float32) * s, 'bq': jnp.zeros((D,), jnp.float32), 'Wk': jax.random.normal(ks[4], (D, D), jnp.float32) * s, 'bk': jnp.zeros((D,), jnp.float32), 'Wv': jax.random.normal(ks[5], (D, D), jnp.float32) * s, 'bv': jnp.zeros((D,), jnp.float32), 'Wo': jax.random.normal(ks[6], (D, D), jnp.float32) * s, 'bo': jnp.zeros((D,), jnp.float32)}
        return inp
    _L0_xattn_all = _L0_xattn_setup()
    _L0_xattn_in = {k: v for k, v in _L0_xattn_all.items() if k in ('Wq', 'bq', 'Wk', 'bk', 'Wv', 'bv', 'Wo', 'bo')}
    del _L0_xattn_all

    def _L0_ffn_setup():
        import jax, jax.numpy as jnp
        import numpy as np
        K_TOP = 2
        key = jax.random.key(seed)
        k1, k2, k3 = jax.random.split(key, 3)
        B, S, H, E = (4, 256, 128, 8)
        hidden_states = jax.random.normal(k1, (B, S, H), dtype=jnp.float32)
        router_w = jax.random.normal(k2, (E, H), dtype=jnp.float32) * 0.02
        expert_weights = jax.random.normal(k3, (E, H, H), dtype=jnp.float32) * 0.02
        return {'hidden_states': hidden_states, 'router_w': router_w, 'expert_weights': expert_weights}
    _L0_ffn_all = _L0_ffn_setup()
    _L0_ffn_in = {k: v for k, v in _L0_ffn_all.items() if k in ('router_w', 'expert_weights')}
    del _L0_ffn_all
    return {'x': x, 'ctx_1024': ctx_1024, 'L0_attn_Wq': _L0_attn_in['Wq'], 'L0_attn_Wk': _L0_attn_in['Wk'], 'L0_attn_Wv': _L0_attn_in['Wv'], 'L0_xattn_Wq': _L0_xattn_in['Wq'], 'L0_xattn_bq': _L0_xattn_in['bq'], 'L0_xattn_Wk': _L0_xattn_in['Wk'], 'L0_xattn_bk': _L0_xattn_in['bk'], 'L0_xattn_Wv': _L0_xattn_in['Wv'], 'L0_xattn_bv': _L0_xattn_in['bv'], 'L0_xattn_Wo': _L0_xattn_in['Wo'], 'L0_xattn_bo': _L0_xattn_in['bo'], 'L0_ffn_router_w': _L0_ffn_in['router_w'], 'L0_ffn_expert_weights': _L0_ffn_in['expert_weights']}

def reference(x, ctx_1024, L0_attn_Wq, L0_attn_Wk, L0_attn_Wv, L0_xattn_Wq, L0_xattn_bq, L0_xattn_Wk, L0_xattn_bk, L0_xattn_Wv, L0_xattn_bv, L0_xattn_Wo, L0_xattn_bo, L0_ffn_router_w, L0_ffn_expert_weights):
    import jax
    import jax.numpy as jnp

    def _L0_attn_ref(x, Wq, Wk, Wv):
        import jax, jax.numpy as jnp
        import numpy as np
        NUM_HEADS = 16

        def _rope_tables(seq_len, head_dim, dtype):
            pos = jnp.arange(seq_len, dtype=jnp.float32)
            inv = jnp.power(10000.0, -2.0 * jnp.arange(head_dim // 2, dtype=jnp.float32) / head_dim)
            ang = pos[:, None] * inv[None, :]
            cos = jnp.repeat(jnp.cos(ang), 2, axis=-1).astype(dtype)
            sin = jnp.repeat(jnp.sin(ang), 2, axis=-1).astype(dtype)
            return (cos[None, None], sin[None, None])

        def _rotate_half_interleaved(x):
            x2 = jnp.stack([-x[..., 1::2], x[..., ::2]], axis=-1)
            return x2.reshape(x.shape)
        B, N, C = x.shape
        H = NUM_HEADS
        D = C // H
        scale = D ** (-0.5)

        def heads(y):
            return y.reshape(B, N, H, D).transpose(0, 2, 1, 3)
        q = heads(x @ Wq.T)
        k = heads(x @ Wk.T)
        v = heads(x @ Wv.T)
        cos, sin = _rope_tables(N, D, x.dtype)
        q = q * cos + _rotate_half_interleaved(q) * sin
        k = k * cos + _rotate_half_interleaved(k) * sin
        attn = jnp.einsum('bhnd,bhmd->bhnm', q, k) * scale
        attn = jax.nn.softmax(attn, axis=-1)
        out = jnp.einsum('bhnm,bhmd->bhnd', attn, v)
        return out.transpose(0, 2, 1, 3).reshape(B, N, C)

    def _L0_xattn_ref(query, key, value, Wq, bq, Wk, bk, Wv, bv, Wo, bo):
        import jax, jax.numpy as jnp
        import numpy as np
        D_MODEL = 128
        NUM_HEADS = 16
        HEAD_DIM = D_MODEL // NUM_HEADS
        B, S, D = query.shape
        H, Hd = (NUM_HEADS, HEAD_DIM)
        Q = (query @ Wq.T + bq).reshape(B, S, H, Hd).transpose(0, 2, 1, 3)
        K = (key @ Wk.T + bk).reshape(B, S, H, Hd).transpose(0, 2, 1, 3)
        V = (value @ Wv.T + bv).reshape(B, S, H, Hd).transpose(0, 2, 1, 3)
        scale = 1.0 / jnp.sqrt(jnp.asarray(Hd, Q.dtype))
        scores = jnp.einsum('bhqd,bhkd->bhqk', Q, K) * scale
        attn = jax.nn.softmax(scores, axis=-1)
        out = jnp.einsum('bhqk,bhkd->bhqd', attn, V)
        out = out.transpose(0, 2, 1, 3).reshape(B, S, D)
        return out @ Wo.T + bo

    def _L0_ffn_ref(hidden_states, router_w, expert_weights):
        import jax, jax.numpy as jnp
        import numpy as np
        K_TOP = 2
        B, S, H = hidden_states.shape
        x = hidden_states.reshape(-1, H)
        logits = x @ router_w.T
        probs = jax.nn.softmax(logits, axis=-1)
        topk_vals, topk_idx = jax.lax.top_k(probs, K_TOP)
        topk_w = topk_vals / (topk_vals.sum(-1, keepdims=True) + 1e-06)
        expert_out = jnp.einsum('nh,eho->eno', x, expert_weights)
        combined = jnp.take_along_axis(expert_out.transpose(1, 0, 2), topk_idx[:, :, None], axis=1)
        combined = combined.transpose(1, 0, 2)
        remap_bias = jnp.take_along_axis(probs, topk_idx, axis=1).T[:, :, None]
        weights = topk_w.T[:, :, None]
        out = ((combined + remap_bias) * weights).sum(axis=0)
        return out.reshape(B, S, H)
    x = x + _L0_attn_ref(_layernorm(x, axis=-1), L0_attn_Wq, L0_attn_Wk, L0_attn_Wv)
    x = x + _L0_xattn_ref(_layernorm(x, axis=-1), ctx_1024, ctx_1024, L0_xattn_Wq, L0_xattn_bq, L0_xattn_Wk, L0_xattn_bk, L0_xattn_Wv, L0_xattn_bv, L0_xattn_Wo, L0_xattn_bo)
    x = x + _L0_ffn_ref(_layernorm(x, axis=-1), L0_ffn_router_w, L0_ffn_expert_weights)
    return x

_drawn_inputs = setup_inputs


def setup_inputs(seed=0):
    import zlib

    import numpy as np

    out = dict(_drawn_inputs(seed))
    spreads = {'L0_xattn_bq': (0.0, 0.1),
     'L0_xattn_bk': (0.0, 0.1),
     'L0_xattn_bv': (0.0, 0.1),
     'L0_xattn_bo': (0.0, 0.1)}
    factors = {}
    for name, (base, spread) in spreads.items():
        noise = np.random.default_rng([zlib.crc32(name.encode()), seed]).standard_normal(out[name].shape)
        drawn = base * np.exp(spread * noise) if base else spread * noise
        out[name] = jnp.asarray(drawn.astype(out[name].dtype))
    for name, factor in factors.items():
        out[name] = (out[name] * factor).astype(out[name].dtype)
    return out
```

```python
from contextlib import ExitStack

import numpy as np

import concourse.bass as bass
from concourse import mybir
from concourse.alu_op_type import AluOpType as ALU

ACT = mybir.ActivationFunctionType
AX = mybir.AxisListType
F32 = mybir.dt.float32
BF16 = mybir.dt.bfloat16

B, N, C = 16, 128, 128
H, D = 16, 8
E = 8
GB = 4
NG = B // GB
TW = GB * N
HALF = H // 2
TERMS = 6
SLOTS = 8
ROWS = TERMS * D
SHIFTED = ROWS + 2
SELF, CROSS, FFN = "self", "cross", "ffn"
LINKS = 14
EPS = 1e-5


class Step:

    def __init__(self, i, c, per=4):
        self.i, self.c, self.per = i, c, per

    def __add__(self, k):
        return Step(self.i, self.c + k, self.per)

    def count(self, per=1, more=0):
        static = per * self.c + more
        return static if self.i is None else self.i * (per * self.per) + static

    def turn(self, per=1, more=0):
        static = per * (self.c // 4) + more
        return static if self.i is None else self.i * per + static

    def slot(self, n):
        return self.c % n


def build(nc, x, ctx_in, wq1, wk1, wv1, wq2, bq2, wk2, bk2, wv2, bv2, wo2, bo2, router, experts,
          ident, order, rotate, cosines, sines, out):
    with ExitStack() as stack:
        def sb(name, shape, dt=F32):
            return stack.enter_context(nc.sbuf_tensor(name, shape, dt))

        def sem(name):
            return stack.enter_context(nc.semaphore(name))

        ps01 = stack.enter_context(nc.psum_tensor("ps01", [128, 2, 512], F32))
        ps23 = stack.enter_context(nc.psum_tensor("ps23", [128, 2, 512], F32))
        ps4 = stack.enter_context(nc.psum_tensor("ps4", [128, 512], F32))
        ps5 = stack.enter_context(nc.psum_tensor("ps5", [128, 512], F32))
        ps6 = stack.enter_context(nc.psum_tensor("ps6", [128, 512], F32))
        ps7 = stack.enter_context(nc.psum_tensor("ps7", [128, 512], F32))

        ident_s, order_s, rotate_s = sb("ident_s", [128, 128]), sb("order_s", [128, 128]), sb("rotate_s", [128, 128])
        ident_b = sb("ident_b", [128, 128], BF16)
        cos_s, sin_s = sb("cos_s", [128, N]), sb("sin_s", [128, N])
        raw = sb("raw", [128, 7, 128])
        wt = sb("wt", [128, 9, 128])
        Q1, RQ1, K1, RK1, V1, Q2, K2, V2, O2 = range(9)
        bqk_raw, bqk = sb("bqk_raw", [128, 2]), sb("bqk", [128, 2])
        brow = sb("brow", [1, 2, 128])
        bvo = sb("bvo", [128, 2, 128])
        ones_row = sb("ones_row", [1, 128])
        router_raw, router_t = sb("router_raw", [E, 128]), sb("router_t", [128, E])
        experts_s = sb("experts_s", [128, E, 128])
        minus_ones = sb("minus_ones", [128, B * N], BF16)
        before = sb("before", [128, E, E])
        minus_half = sb("minus_half", [128, B])
        zeros = sb("zeros", [128, HALF * D])

        hid = sb("hid", [128, B, C])
        context = sb("context", [128, B, C])
        stats = sb("stats", [128, B, 6])
        mean, rstd = sb("mean", [128, B]), sb("rstd", [128, B])
        ln_a, ln_b, ln_c, ln_d, ln_e, ln_f = (sb(f"ln_{n}", [128, B]) for n in "abcdef")
        xh = sb("xh", [128, GB, C])
        cg = sb("cg", [128, GB, C])
        xt, ct = sb("xt", [128, TW]), sb("ct", [128, TW])
        rope_a = [sb(f"rope_a{o}", [128, TW]) for o in range(2)]
        rope_b = [sb(f"rope_b{o}", [128, TW]) for o in range(2)]
        full = [sb(f"full{o}", [128, TW]) for o in range(2)]
        rest = [sb(f"rest{o}", [128, TW]) for o in range(2)]
        part = [sb(f"part{o}", [128, 3, TW], BF16) for o in range(2)]
        vall = sb("vall", [128, B, C])
        qst = [sb(f"qst{q}", [128, HALF, N], BF16) for q in range(4)]
        kst = [sb(f"kst{q}", [128, HALF, N], BF16) for q in range(4)]
        smax = [sb(f"smax{q}", [128, 2, HALF]) for q in range(2)]
        shift = [sb(f"shift{q}", [128, 2, 2, HALF], BF16) for q in range(2)]
        shift_t = [sb(f"shift_t{q}", [4 * HALF, N], BF16) for q in range(2)]
        probs = [sb(f"probs{q}", [128, 2, 2, 4, N]) for q in range(2)]
        vpad = [sb(f"vpad{q}", [128, HALF, 2, 32]) for q in range(2)]
        ot = [sb(f"ot{q}", [128, 2, N]) for q in range(2)]
        rsum = [sb(f"rsum{q}", [128, H]) for q in range(2)]
        att = [sb(f"att{q}", [128, H, D]) for q in range(2)]
        att_t = [sb(f"att_t{q}", [128, N]) for q in range(2)]
        xt_all = sb("xt_all", [128, B, N])
        gate = sb("gate", [128, B, E])
        gbias = sb("gbias", [128, B])
        g_l, g_p, g_w, g_q, g_r = (sb(f"g_{n}", [128, GB, E]) for n in "lpwqr")
        g_gt, g_eq, g_lo = (sb(f"g_{n}", [128, GB, E, E]) for n in ("gt", "eq", "lo"))
        g_s = sb("g_s", [128, 6, GB])
        xe = [sb(f"xe{q}", [128, N]) for q in range(2)]
        acc = [[sb(f"acc{q}{h}", [128, C]) for h in range(2)] for q in range(2)]
        result = sb("result", [128, B, C])

        scratch = [nc.dram_tensor(f"scratch{o}", [NG, 2, SLOTS, 64, TW], BF16).ap() for o in range(2)]

        const_in, weights_in, x_in, ctx_in_done, experts_in = (
            sem(n) for n in ("const_in", "weights_in", "x_in", "ctx_in_done", "experts_in"))
        pool_const, dve_const, w_ps, w_sb, minus_ones_out = (
            sem(n) for n in ("pool_const", "dve_const", "w_ps", "w_sb", "minus_ones_out"))
        x_stats = sem("x_stats")
        ln_step = {k: sem(f"ln_step_{k}") for k in (SELF, CROSS, FFN)}
        rstd_done = {k: sem(f"rstd_done_{k}") for k in (SELF, CROSS, FFN)}
        PROJECT = ("xh_done",
                   "x_ps",
                   "x_sb",
                   "proj",
                   "q_read", "k_read",
                   "q_full", "k_full",
                   "part1", "rest", "part2", "part3",
                   "v_sb",
                   "q_out", "k_out")
        ATTEND = ("s_ps", "max_done",
                  "shift_hi", "shift_done", "shift_ps", "shift_sb",
                  "r_ps", "exp_done",
                  "vpad_done", "pv",
                  "ot_sb", "ot_ps",
                  "rsum_done", "att_done",
                  "att_ps", "att_sb", "y_ps", "bias_done",
                  "hid_done", "stat_done")
        S = {(ph, n): sem(f"{ph}_{n}") for ph in (SELF, CROSS) for n in PROJECT + ATTEND}
        stack_in = {(ph, q): sem(f"{ph}_stack_in{q}") for ph in (SELF, CROSS) for q in range(4)}
        shift_in = {(ph, q): sem(f"{ph}_shift_in{q}") for ph in (SELF, CROSS) for q in range(4)}
        (f_xh, f_xps, f_xsb, f_logits, f_logits_read, f_exp, f_link, f_gate,
         f_xe, f_y, f_acc, f_result, f_out) = (
            sem(f"ffn_{n}") for n in ("xh", "x_ps", "x_sb", "logits", "logits_read", "exp", "link", "gate",
                                      "xe", "y", "acc", "result", "out"))

        def need(eng, s, value):
            if not (isinstance(value, int) and value <= 0):
                eng.wait_ge(s, value)

        def groups(eng, body):
            body(Step(None, 0, 1))
            with eng.Fori(1, NG) as i:
                body(Step(i, 0, 1))

        def steps(eng, body):
            for c in range(-2, GB):
                body(Step(None, c))
            with eng.Fori(1, NG - 1) as i:
                for c in range(GB):
                    body(Step(i, c))
            for c in range(B - GB, B + 4):
                body(Step(None, c))

        def tiles(eng, front, expert):
            front(Step(None, 0, 1))
            front(Step(None, 1, 1))
            for c in range(GB):
                expert(Step(None, c))
            with eng.Fori(1, NG - 1) as i:
                front(Step(i, 1, 1))
                for c in range(GB):
                    expert(Step(i, c))
            for c in range(B - GB, B):
                expert(Step(None, c))

        def live(b):
            return b.i is not None or 0 <= b.c < B

        def of_group(t, g):
            return t[:, bass.ds(g.count(GB), GB)]

        def batches(ap):
            return ap.rearrange("p (b n) -> p b n", b=GB)

        block = stack.enter_context(nc.Block())

        @block.sync
        def _(sp):
            for dst, src in ((ident_s, ident), (order_s, order), (rotate_s, rotate), (cos_s, cosines), (sin_s, sines)):
                sp.dma_start(dst[:, :], src).then_inc(const_in, 16)
            for n, w in enumerate((wq1, wk1, wv1, wq2, wk2, wv2, wo2)):
                sp.dma_start(raw[:, n, :], w).then_inc(weights_in, 16)
            for n, v in enumerate((bq2, bk2)):
                sp.dma_start(bqk_raw[:, n:n + 1], v.rearrange("(c a) -> c a", a=1)).then_inc(weights_in, 16)
            for n, v in enumerate((bv2, bo2)):
                sp.dma_start(brow[:, n, :], v.rearrange("(a c) -> a c", a=1)).then_inc(weights_in, 16)
            sp.dma_start(router_raw[:, :], router).then_inc(weights_in, 16)
            sp.dma_start(context[:, :, :], ctx_in.rearrange("b n c -> n b c")).then_inc(ctx_in_done, 16)
            sp.dma_start(experts_s[:, :, :], experts.rearrange("e h o -> h e o")).then_inc(experts_in, 16)
            sp.wait_ge(pool_const, 1)
            for o in range(2):
                for a in range(2):
                    sp.dma_start(scratch[o][:, a, TERMS:SLOTS].rearrange("g t c n -> (t c) g n"),
                                 minus_ones[:, :].rearrange("c (g n) -> c g n", g=NG)).then_inc(minus_ones_out, 16)

            def store_parts(ph, g):
                for o, stored in enumerate(("q_out", "k_out")):
                    sp.wait_ge(S[ph, "part2"], g.count(2, o + 1))
                    sp.wait_ge(S[ph, "part3"], g.count(2, o + 1))
                    for n, (first, count) in enumerate(((0, 3), (3, 2), (5, 1))):
                        src = part[0][:, 0:count, :] if o == 0 else part[1][:, n:n + 1, :].broadcast_to([128, count, TW])
                        for a in range(2):
                            dst = scratch[o][g.count(1), a, first:first + count].rearrange("t c n -> c t n")
                            sp.dma_start(dst, src[64 * a:64 * a + 64, :, :]).then_inc(S[ph, stored], 16)

            def attend(ph):
                def load(b):
                    for o, dst in enumerate((qst, kst)):
                        src = scratch[o][b.turn()].rearrange("a t (d p) (b n) -> (a t d) p b n", d=D, b=GB)
                        sp.dma_start(dst[b.slot(4)][:, :, :], src[:, :, b.slot(4), :]).then_inc(
                            stack_in[ph, b.slot(4)], 16)

                sp.wait_ge(S[ph, "q_out"], 16 * TERMS * NG)
                sp.wait_ge(S[ph, "k_out"], 16 * TERMS * NG)
                if ph == SELF:
                    sp.wait_ge(minus_ones_out, 16 * 4)
                for c in range(4):
                    load(Step(None, c))

                def step(t):
                    b = t + 1
                    if live(b):
                        sp.wait_ge(S[ph, "shift_sb"], b.count(1, 1))
                        for a in range(2):
                            rows = slice(64 * a + ROWS, 64 * a + SHIFTED)
                            sp.dma_start(qst[b.slot(4)][rows, :, :].rearrange("r p n -> r (p n)"),
                                         shift_t[b.slot(2)][2 * HALF * a:2 * HALF * (a + 1), :]).then_inc(
                                shift_in[ph, b.slot(4)], 16)
                    if live(t) and live(t + 4):
                        sp.wait_ge(S[ph, "r_ps"], t.count(2, 2))
                        load(t + 4)

                steps(sp, step)

            for ph in (SELF, CROSS):
                groups(sp, lambda g: store_parts(ph, g))
                attend(ph)

            for g in range(NG):
                own = slice(GB * g, GB * (g + 1))
                sp.wait_ge(f_result, GB * (g + 1))
                sp.dma_start(out[own].rearrange("b n c -> n b c"), result[:, own, :]).then_inc(f_out, 16)
            sp.wait_ge(f_out, 16 * NG)

        @block.tensor
        def _(pe):
            pe.wait_ge(const_in, 16 * 5)
            pe.wait_ge(weights_in, 16 * 12)
            pe.wait_ge(dve_const, 2)
            plan = ((Q1, 0, order_s), (RQ1, 0, rotate_s), (K1, 1, order_s), (RK1, 1, rotate_s), (V1, 2, ident_s),
                    (Q2, 3, order_s), (K2, 4, order_s), (V2, 5, ident_s), (O2, 6, ident_s))
            for n, src, turn in plan:
                dst = (ps01[:, 0], ps01[:, 1], ps23[:, 0])[n // 4]
                pe.matmul(dst[:, 128 * (n % 4):128 * (n % 4) + 128], raw[:, src, :], turn[:, :], start=True, stop=True)
            pe.matmul(ps4[:, 0:2], order_s[:, :], bqk_raw[:, :], start=True, stop=True)
            pe.matmul(ps4[:, 8:8 + E], router_raw[:, :], ident_s[0:E, 0:E], start=True, stop=True)
            pe.matmul(ps4[:, 128:384], ones_row[:, :], brow[:, :, :].rearrange("a b c -> a (b c)"),
                      start=True, stop=True).then_inc(w_ps, 1)
            pe.wait_ge(w_sb, 1)

            def project(ph, g):
                pe.wait_ge(S[ph, "xh_done"], g.count(1, 1))
                need(pe, S[ph, "x_sb"], g.count(1))
                for j in range(GB):
                    last = pe.transpose(ps5[:, N * j:N * j + N], xh[:, j, :], ident_s[:, :])
                    if ph == CROSS:
                        last = pe.transpose(ps6[:, N * j:N * j + N], cg[:, j, :], ident_s[:, :])
                last.then_inc(S[ph, "x_ps"], 1)
                w_q, w_k, w_v = (Q1, K1, V1) if ph == SELF else (Q2, K2, V2)
                src = xt if ph == SELF else ct
                pe.wait_ge(S[ph, "x_sb"], g.count(1, 1))
                need(pe, S[ph, "q_read"], g.count(1))
                last = pe.matmul(ps01[:, 0], wt[:, w_q, :], xt[:, :], start=True, stop=True)
                if ph == SELF:
                    last = pe.matmul(ps01[:, 1], wt[:, RQ1, :], xt[:, :], start=True, stop=True)
                last.then_inc(S[ph, "proj"], 1)
                need(pe, S[ph, "k_read"], g.count(1))
                last = pe.matmul(ps23[:, 0], wt[:, w_k, :], src[:, :], start=True, stop=True)
                if ph == SELF:
                    last = pe.matmul(ps23[:, 1], wt[:, RK1, :], src[:, :], start=True, stop=True)
                last.then_inc(S[ph, "proj"], 1)
                need(pe, S[ph, "v_sb"], g.count(1))
                for j in range(GB):
                    last = pe.matmul(ps4[:, C * j:C * j + C], src[:, N * j:N * j + N], wt[:, w_v, :], start=True, stop=True)
                last.then_inc(S[ph, "proj"], 1)

            def attend(ph):
                def scores(b, u):
                    q = b.slot(4)
                    if u == 0:
                        pe.wait_ge(stack_in[ph, q], b.turn(32, 32))
                    need(pe, S[ph, "max_done"], b.count(2, u))
                    for p in range(4 * u, 4 * u + 4):
                        for a in range(2):
                            rows = slice(64 * a, 64 * a + ROWS)
                            last = pe.matmul(ps01[:, a, N * (p % 4):N * (p % 4) + N], qst[q][rows, p, :], kst[q][rows, p, :],
                                             start=True, stop=True)
                    last.then_inc(S[ph, "s_ps"], 1)

                def shifted(b, u):
                    q = b.slot(4)
                    if u == 0:
                        pe.wait_ge(shift_in[ph, q], b.turn(32, 32))
                    need(pe, S[ph, "exp_done"], b.count(2, u))
                    for p in range(4 * u, 4 * u + 4):
                        for a in range(2):
                            rows = slice(64 * a, 64 * a + SHIFTED)
                            last = pe.matmul(ps23[:, a, N * (p % 4):N * (p % 4) + N], kst[q][rows, p, :], qst[q][rows, p, :],
                                             start=True, stop=True)
                    last.then_inc(S[ph, "r_ps"], 1)

                def weigh(b, r):
                    if r == 0:
                        pe.wait_ge(S[ph, "exp_done"], b.count(2, 2))
                        pe.wait_ge(S[ph, "vpad_done"], b.count(1, 1))
                        need(pe, S[ph, "ot_sb"], b.count(1))
                    for s in range(2):
                        for j in range(4):
                            p = 2 * j + s
                            last = pe.matmul(ps4[32 * j:32 * j + 32, N * r:N * r + N], vpad[b.slot(2)][:, 4 * r + j, s, :],
                                             probs[b.slot(2)][:, p // 4, r, p % 4, :], start=(s == 0), stop=(s == 1),
                                             tile_position=(0, 32 * j))
                    if r == 1:
                        last.then_inc(S[ph, "pv"], 1)

                def step(t):
                    if live(t + 2):
                        scores(t + 2, 0)
                    b = t + -2
                    if live(b):
                        pe.wait_ge(S[ph, "ot_sb"], b.count(1, 1))
                        need(pe, S[ph, "att_done"], b.count(1))
                        for r in range(2):
                            last = pe.transpose(ps6[:, N * r:N * r + N], ot[b.slot(2)][:, r, :], ident_s[:, :])
                        last.then_inc(S[ph, "ot_ps"], 1)
                    b = t + -3
                    if ph == CROSS and live(b):
                        pe.wait_ge(S[ph, "att_done"], b.count(1, 1))
                        need(pe, S[ph, "hid_done"], b.count(1))
                        pe.transpose(ps7[:, 0:N], att[b.slot(2)][:, :, :].rearrange("n h d -> n (h d)"),
                                     ident_s[:, :]).then_inc(S[ph, "att_ps"], 1)
                    if live(t):
                        shifted(t, 0)
                    b = t + 1
                    if live(b):
                        pe.wait_ge(S[ph, "shift_done"], b.count(1, 1))
                        need(pe, S[ph, "shift_sb"], b.count(1))
                        pe.transpose(ps5[0:4 * HALF, 0:N // 2].bitcast(BF16),
                                     shift[b.slot(2)][:, :, :, :].rearrange("n a s p -> n (a s p)"),
                                     ident_b[:, :]).then_inc(S[ph, "shift_ps"], 1)
                    if live(t + -1):
                        weigh(t + -1, 0)
                    if live(t + 2):
                        scores(t + 2, 1)
                    if live(t):
                        shifted(t, 1)
                    b = t + -3
                    if ph == CROSS and live(b):
                        pe.wait_ge(S[ph, "att_sb"], b.count(1, 1))
                        pe.matmul(ps7[:, N:N + C], att_t[b.slot(2)][:, :], wt[:, O2, :], start=True,
                                  stop=True).then_inc(S[ph, "y_ps"], 1)
                    if live(t + -1):
                        weigh(t + -1, 1)

                steps(pe, step)

            for ph in (SELF, CROSS):
                groups(pe, lambda g: project(ph, g))
                attend(ph)

            def front(g):
                pe.wait_ge(f_xh, g.count(1, 1))
                need(pe, f_xsb, g.count(1))
                for j in range(GB):
                    last = pe.transpose(ps5[:, N * j:N * j + N], xh[:, j, :], ident_s[:, :])
                last.then_inc(f_xps, 1)
                pe.wait_ge(f_xsb, g.count(1, 1))
                need(pe, f_logits_read, g.count(1))
                for j in range(GB):
                    last = pe.matmul(ps6[:, E * j:E * j + E], xt[:, N * j:N * j + N], router_t[:, :], start=True, stop=True)
                last.then_inc(f_logits, 1)

            def expert(b):
                y = (ps01, ps23)[b.slot(2)]
                pe.wait_ge(f_xe, b.count(1, 1))
                need(pe, f_acc, b.count(8, -8))
                for h in range(2):
                    last = pe.matmul(y[:, h], xe[b.slot(2)][:, :],
                                     experts_s[:, 4 * h:4 * h + 4, :].rearrange("h e o -> h (e o)"), start=True, stop=True)
                last.then_inc(f_y, 1)

            pe.wait_ge(experts_in, 16)
            tiles(pe, front, expert)

        @block.scalar
        def _(act):
            act.dma_start(hid[:, :, :], x.rearrange("b n c -> n b c")).then_inc(x_in, 16)
            act.wait_ge(w_ps, 1)
            for n in range(2):
                nc.scalar.copy(wt[:, 4 * n:4 * n + 4, :].rearrange("i n o -> i (n o)"), ps01[:, n])
            nc.scalar.copy(wt[:, 8, :], ps23[:, 0, 0:128])
            nc.scalar.copy(bqk[:, :], ps4[:, 0:2])
            nc.scalar.copy(router_t[:, :], ps4[:, 8:8 + E])
            nc.scalar.copy(bvo[:, :, :].rearrange("n a c -> n (a c)"), ps4[:, 128:384]).then_inc(w_sb, 1)
            act.wait_ge(w_sb, 1)

            def project(ph, g):
                act.wait_ge(S[ph, "x_ps"], g.count(1, 1))
                need(act, S[ph, "proj"], g.count(3))
                last = nc.scalar.copy(xt[:, :], ps5[:, :])
                if ph == CROSS:
                    last = nc.scalar.copy(ct[:, :], ps6[:, :])
                last.then_inc(S[ph, "x_sb"], 1)
                for o, (read, whole, stored) in enumerate((("q_read", "q_full", "q_out"), ("k_read", "k_full", "k_out"))):
                    if ph == CROSS:
                        act.wait_ge(S[ph, "proj"], g.count(3, o + 1))
                        need(act, S[ph, "rest"], g.count(2, o - 1))
                        nc.scalar.activation(full[o][:, :], (ps01, ps23)[o][:, 0], ACT.Identity,
                                             bias=bqk[:, o:o + 1]).then_inc(S[ph, read], 1)
                        act.wait_ge(S[ph, read], g.count(1, 1))
                    else:
                        act.wait_ge(S[ph, whole], g.count(1, 1))
                    need(act, S[ph, stored], g.count(16 * TERMS))
                    nc.scalar.copy(part[o][:, 0, :], full[o][:, :]).then_inc(S[ph, "part1"], 1)
                if ph == SELF:
                    act.wait_ge(S[ph, "proj"], g.count(3, 3))
                    nc.scalar.copy(of_group(vall, g), batches(ps4[:, :])).then_inc(S[ph, "v_sb"], 1)
                for o in range(2):
                    act.wait_ge(S[ph, "rest"], g.count(2, o + 1))
                    nc.scalar.copy(part[o][:, 1, :], rest[o][:, :]).then_inc(S[ph, "part2"], 1)

            def attend(ph):
                def exponentials(b, u):
                    act.wait_ge(S[ph, "r_ps"], b.count(2, u + 1))
                    if u == 0:
                        need(act, S[ph, "pv"], b.count(1, -1))
                    nc.scalar.activation(probs[b.slot(2)][:, u, :, :, :].rearrange("m a p n -> m (a p n)"),
                                         ps23[:, :, :].rearrange("m a n -> m (a n)"), ACT.Exp,
                                         scale=D ** -0.5).then_inc(S[ph, "exp_done"], 1)

                def step(t):
                    if live(t):
                        exponentials(t, 0)
                    b = t + 1
                    if live(b):
                        act.wait_ge(S[ph, "shift_ps"], b.count(1, 1))
                        old = b + -2
                        if live(old):
                            act.wait_ge(shift_in[ph, old.slot(4)], old.turn(32, 32))
                        nc.scalar.copy(shift_t[b.slot(2)][:, :], ps5[0:4 * HALF, 0:N // 2].bitcast(BF16)).then_inc(
                            S[ph, "shift_sb"], 1)
                    b = t + -3
                    if ph == CROSS and live(b):
                        act.wait_ge(S[ph, "att_ps"], b.count(1, 1))
                        need(act, S[ph, "y_ps"], b.count(1, -1))
                        nc.scalar.copy(att_t[b.slot(2)][:, :], ps7[:, 0:N]).then_inc(S[ph, "att_sb"], 1)
                    if live(t):
                        exponentials(t, 1)
                    b = t + -1
                    if live(b):
                        act.wait_ge(S[ph, "pv"], b.count(1, 1))
                        need(act, S[ph, "ot_ps"], b.count(1, -1))
                        nc.scalar.copy(ot[b.slot(2)][:, :, :].rearrange("c r n -> c (r n)"), ps4[:, 0:2 * N]).then_inc(
                            S[ph, "ot_sb"], 1)

                steps(act, step)

            for ph in (SELF, CROSS):
                groups(act, lambda g: project(ph, g))
                attend(ph)

            def front(g):
                act.wait_ge(f_xps, g.count(1, 1))
                need(act, f_logits, g.count(1))
                nc.scalar.copy(xt[:, :], ps5[:, :])
                nc.scalar.copy(of_group(xt_all, g), batches(ps5[:, :])).then_inc(f_xsb, 1)
                act.wait_ge(f_logits_read, g.count(1, 1))
                nc.scalar.activation(g_p[:, :, :], g_l[:, :, :], ACT.Exp).then_inc(f_exp, 1)

            def expert(b):
                act.wait_ge(f_xsb, b.turn(1, 1))
                need(act, f_y, b.count(1, -1))
                nc.scalar.copy(xe[b.slot(2)][:, :], xt_all[:, b.count(), :]).then_inc(f_xe, 1)

            tiles(act, front, expert)

        @block.vector
        def _(dve):
            nc.vector.memset(ones_row[:, :], 1.0).then_inc(dve_const, 1)
            dve.wait_ge(const_in, 16 * 5)
            nc.vector.tensor_copy(ident_b[:, :], ident_s[:, :]).then_inc(dve_const, 1)
            dve.wait_ge(x_in, 16)
            for b in range(B):
                nc.vector.bn_stats(stats[:, b, :], hid[:, b, :]).then_inc(x_stats, 1)

            def layernorm(done, k):
                ln = ln_step[k]
                dve.wait_ge(done, B)
                nc.vector.tensor_tensor(ln_a[:, :], stats[:, :, 1], stats[:, :, 4], ALU.add).then_inc(ln, 1)
                nc.vector.tensor_tensor(ln_b[:, :], stats[:, :, 1], stats[:, :, 4], ALU.subtract).then_inc(ln, 1)
                nc.vector.tensor_tensor(ln_c[:, :], stats[:, :, 2], stats[:, :, 5], ALU.add).then_inc(ln, 1)
                dve.wait_ge(ln, 3)
                nc.vector.tensor_scalar(mean[:, :], ln_a[:, :], 0.5, None, ALU.mult).then_inc(ln, 1)
                nc.vector.scalar_tensor_tensor(ln_d[:, :], ln_b[:, :], 0.25, ln_b[:, :], ALU.mult, ALU.mult).then_inc(ln, 1)
                dve.wait_ge(ln, 5)
                nc.vector.scalar_tensor_tensor(ln_e[:, :], ln_c[:, :], 1.0 / C, ln_d[:, :], ALU.mult, ALU.add).then_inc(ln, 1)
                dve.wait_ge(ln, 6)
                nc.vector.tensor_scalar(ln_f[:, :], ln_e[:, :], EPS, None, ALU.add).then_inc(ln, 1)
                dve.wait_ge(rstd_done[k], 1)

            def normalise(g, last_read, done):
                need(dve, last_read, g.count(1))
                for j in range(GB):
                    b = g.count(GB, j)
                    last = nc.vector.tensor_scalar(xh[:, j, :], hid[:, b, :], mean[:, bass.ds(b, 1)], rstd[:, bass.ds(b, 1)],
                                                   ALU.subtract, ALU.mult)
                if done is not None:
                    last.then_inc(done, 1)

            def project(ph, g):
                if ph == CROSS:
                    normalise(g, S[ph, "x_ps"], None)
                    nc.vector.tensor_copy(cg[:, :, :], of_group(context, g)).then_inc(S[ph, "xh_done"], 1)
                    dve.wait_ge(S[ph, "proj"], g.count(3, 3))
                    nc.vector.tensor_tensor(of_group(vall, g), batches(ps4[:, :]), bvo[:, 0:1, :].broadcast_to([128, GB, C]),
                                            ALU.add).then_inc(S[ph, "v_sb"], 1)
                    return
                normalise(g, S[ph, "x_ps"], S[ph, "xh_done"])
                cos_g = cos_s[:, :].unsqueeze(1).broadcast_to([128, GB, N])
                sin_g = sin_s[:, :].unsqueeze(1).broadcast_to([128, GB, N])
                for o, (ps, read, whole) in enumerate(((ps01, "q_read", "q_full"), (ps23, "k_read", "k_full"))):
                    dve.wait_ge(S[ph, "proj"], g.count(3, o + 1))
                    need(dve, S[ph, whole], g.count(1))
                    nc.vector.tensor_tensor(batches(rope_a[o][:, :]), batches(ps[:, 0]), cos_g, ALU.mult)
                    nc.vector.tensor_tensor(batches(rope_b[o][:, :]), batches(ps[:, 1]), sin_g, ALU.mult).then_inc(S[ph, read], 1)
                    if o == 0:
                        dve.wait_ge(S[ph, read], g.count(1, 1))
                        need(dve, S[ph, "rest"], g.count(2, -1))
                        nc.vector.tensor_tensor(full[0][:, :], rope_a[0][:, :], rope_b[0][:, :], ALU.add).then_inc(S[ph, whole], 1)

            def attend(ph):
                def maxima(b, u):
                    dve.wait_ge(S[ph, "s_ps"], b.count(2, u + 1))
                    if u == 0:
                        need(dve, S[ph, "shift_done"], b.count(1, -1))
                    nc.vector.tensor_reduce(smax[b.slot(2)][:, :, 4 * u:4 * u + 4],
                                            ps01[:, :, :].rearrange("n a (p m) -> n a p m", p=4), AX.X,
                                            ALU.max).then_inc(S[ph, "max_done"], 1)

                def step(t):
                    if live(t + 2):
                        maxima(t + 2, 0)
                    b = t + -2
                    if live(b):
                        q = b.slot(2)
                        heads = ps6[:, 0:2 * N].rearrange("n (h e) -> n h e", h=H)
                        dve.wait_ge(S[ph, "ot_ps"], b.count(1, 1))
                        nc.vector.reciprocal(rsum[q][:, :].unsqueeze(2), heads[:, :, D:D + 1]).then_inc(S[ph, "rsum_done"], 1)
                        dve.wait_ge(S[ph, "rsum_done"], b.count(1, 1))
                        need(dve, S[ph, "hid_done" if ph == SELF else "att_ps"], b.count(1, -1))
                        nc.vector.tensor_tensor(att[q][:, :, :], heads[:, :, 0:D],
                                                rsum[q][:, :].unsqueeze(2).broadcast_to([128, H, D]),
                                                ALU.mult).then_inc(S[ph, "att_done"], 1)
                    if live(t + 2):
                        maxima(t + 2, 1)
                    b = t + -3
                    if ph == CROSS and live(b):
                        dve.wait_ge(S[ph, "y_ps"], b.count(1, 1))
                        dve.wait_ge(S[ph, "bias_done"], b.count(1, 1))
                        nc.vector.tensor_tensor(hid[:, b.count(), :], ps7[:, N:N + C], hid[:, b.count(), :],
                                                ALU.add).then_inc(S[ph, "hid_done"], 1)
                    b = t + (-3 if ph == SELF else -4)
                    if live(b):
                        dve.wait_ge(S[ph, "hid_done"], b.count(1, 1))
                        nc.vector.bn_stats(stats[:, b.count(), :], hid[:, b.count(), :]).then_inc(S[ph, "stat_done"], 1)

                steps(dve, step)

            layernorm(x_stats, SELF)
            groups(dve, lambda g: project(SELF, g))
            attend(SELF)
            layernorm(S[SELF, "stat_done"], CROSS)
            dve.wait_ge(ctx_in_done, 16)
            groups(dve, lambda g: project(CROSS, g))
            attend(CROSS)
            layernorm(S[CROSS, "stat_done"], FFN)
            dve.wait_ge(pool_const, 3)

            def front(g):
                links = []

                def link(ins):
                    links.append(ins)
                    ins.then_inc(f_link, 1)
                    dve.wait_ge(f_link, g.count(LINKS, len(links)))

                logits = ps6[:, 0:GB * E].rearrange("n (b e) -> n b e", b=GB)
                per_tile = lambda k: g_s[:, k, :].unsqueeze(2).broadcast_to([128, GB, E])
                other = g_q[:, :, :].unsqueeze(2).broadcast_to([128, GB, E, E])
                mine = g_q[:, :, :].unsqueeze(3).broadcast_to([128, GB, E, E])
                normalise(g, f_xps, f_xh)
                dve.wait_ge(f_logits, g.count(1, 1))
                link(nc.vector.tensor_reduce(g_s[:, 0, :], logits, AX.X, ALU.max))
                nc.vector.tensor_tensor(g_l[:, :, :], logits, per_tile(0), ALU.subtract).then_inc(f_logits_read, 1)
                dve.wait_ge(f_exp, g.count(1, 1))
                link(nc.vector.tensor_reduce(g_s[:, 1, :], g_p[:, :, :], AX.X, ALU.add))
                link(nc.vector.reciprocal(g_s[:, 2, :], g_s[:, 1, :]))
                link(nc.vector.tensor_tensor(g_q[:, :, :], g_p[:, :, :], per_tile(2), ALU.mult))
                nc.vector.tensor_tensor(g_gt[:, :, :, :], other, mine, ALU.is_gt)
                link(nc.vector.tensor_tensor(g_eq[:, :, :, :], other, mine, ALU.is_equal))
                link(nc.vector.tensor_tensor(g_lo[:, :, :, :], g_eq[:, :, :, :],
                                             before[:, :, :].unsqueeze(1).broadcast_to([128, GB, E, E]), ALU.mult))
                link(nc.vector.tensor_tensor(g_eq[:, :, :, :], g_gt[:, :, :, :], g_lo[:, :, :, :], ALU.add))
                link(nc.vector.tensor_reduce(g_r[:, :, :], g_eq[:, :, :, :], AX.X, ALU.add))
                link(nc.vector.scalar_tensor_tensor(g_w[:, :, :], g_r[:, :, :], 1.5, g_q[:, :, :], ALU.is_lt, ALU.mult))
                link(nc.vector.tensor_reduce(g_s[:, 3, :], g_w[:, :, :], AX.X, ALU.add))
                link(nc.vector.tensor_scalar(g_s[:, 4, :], g_s[:, 3, :], 1e-6, None, ALU.add))
                link(nc.vector.reciprocal(g_s[:, 5, :], g_s[:, 4, :]))
                link(nc.vector.tensor_tensor(of_group(gate, g), g_w[:, :, :], per_tile(5), ALU.mult))
                link(nc.vector.tensor_tensor(g_r[:, :, :], of_group(gate, g), g_q[:, :, :], ALU.mult))
                nc.vector.tensor_reduce(of_group(gbias, g), g_r[:, :, :], AX.X, ALU.add).then_inc(f_gate, 1)
                assert len(links) == LINKS

            def expert(b):
                q, k = b.slot(2), b.count()
                dve.wait_ge(f_y, b.count(1, 1))
                dve.wait_ge(f_gate, b.turn(1, 1))
                need(dve, f_result, b.count(1, -1))
                for e in range(4):
                    for h in range(2):
                        y = (ps01, ps23)[q][:, h, C * e:C * e + C]
                        w = gate[:, k, 4 * h + e:4 * h + e + 1]
                        sums = acc[q][h]
                        if e:
                            dve.wait_ge(f_acc, b.count(8, 2 * e + h - 1))
                            ins = nc.vector.scalar_tensor_tensor(sums[:, :], y, w, sums[:, :], ALU.mult, ALU.add)
                        elif h == 0:
                            ins = nc.vector.scalar_tensor_tensor(sums[:, :], y, w, hid[:, k, :], ALU.mult, ALU.add)
                        else:
                            ins = nc.vector.tensor_scalar(sums[:, :], y, w, gbias[:, bass.ds(k, 1)], ALU.mult, ALU.add)
                        ins.then_inc(f_acc, 1)

            tiles(dve, front, expert)

        @block.gpsimd
        def _(pool):
            nc.gpsimd.memset(zeros[:, :], 0.0)
            nc.gpsimd.memset(minus_ones[:, :], -1.0).then_inc(pool_const, 1)
            nc.gpsimd.memset(minus_half[:, :], -0.5)
            for q in range(2):
                nc.gpsimd.memset(vpad[q][:, :, :, :], 0.0)
            nc.gpsimd.memset(before[:, :, :], 0.0).then_inc(pool_const, 1)
            pool.wait_ge(pool_const, 2)
            for q in range(2):
                for s in range(2):
                    nc.gpsimd.memset(vpad[q][:, :, s, 2 * D * s + D:2 * D * s + 2 * D], 1.0)
            for e in range(1, E):
                last = nc.gpsimd.memset(before[:, e, 0:e], 1.0)
            last.then_inc(pool_const, 1)
            pool.wait_ge(pool_const, 3)

            def root(k):
                pool.wait_ge(ln_step[k], 7)
                nc.gpsimd.tensor_tensor(rstd[:, :], ln_f[:, :], minus_half[:, :], ALU.pow).then_inc(rstd_done[k], 1)

            def project(ph, g):
                def less_first(o):
                    pool.wait_ge(S[ph, "part1"], g.count(2, o + 1))
                    need(pool, S[ph, "part2"], g.count(2, o - 1))
                    nc.gpsimd.tensor_tensor(rest[o][:, :], full[o][:, :], part[o][:, 0, :], ALU.subtract).then_inc(S[ph, "rest"], 1)

                less_first(0)
                if ph == SELF:
                    pool.wait_ge(S[ph, "k_read"], g.count(1, 1))
                    nc.gpsimd.tensor_tensor(full[1][:, :], rope_a[1][:, :], rope_b[1][:, :], ALU.add).then_inc(S[ph, "k_full"], 1)
                less_first(1)
                for o in range(2):
                    pool.wait_ge(S[ph, "part2"], g.count(2, o + 1))
                    pool.wait_ge(S[ph, "rest"], g.count(2, o + 1))
                    nc.gpsimd.tensor_tensor(part[o][:, 2, :], rest[o][:, :], part[o][:, 1, :], ALU.subtract).then_inc(S[ph, "part3"], 1)

            def attend(ph):
                pool.wait_ge(S[ph, "v_sb"], NG)
                pool.wait_ge(S[ph, "xh_done"], NG)

                def step(t):
                    b = t
                    if live(b):
                        need(pool, S[ph, "pv"], b.count(1, -1))
                        values = vall[:, b.count(), :].rearrange("m (j s d) -> m j s d", s=2, d=D)
                        for s in range(2):
                            last = nc.gpsimd.tensor_tensor(vpad[b.slot(2)][:, :, s, 2 * D * s:2 * D * s + D], values[:, :, s, :],
                                                           zeros[:, :].rearrange("n (j d) -> n j d", j=HALF), ALU.add)
                        last.then_inc(S[ph, "vpad_done"], 1)
                    b = t + -2
                    if live(b):
                        row = hid[:, b.count(), :]
                        if ph == SELF:
                            pool.wait_ge(S[ph, "att_done"], b.count(1, 1))
                            nc.gpsimd.tensor_tensor(row, att[b.slot(2)][:, :, :].rearrange("n h d -> n (h d)"), row,
                                                    ALU.add).then_inc(S[ph, "hid_done"], 1)
                        else:
                            nc.gpsimd.tensor_tensor(row, bvo[:, 1, :], row, ALU.add).then_inc(S[ph, "bias_done"], 1)
                    b = t + 2
                    if live(b):
                        q = b.slot(2)
                        pool.wait_ge(S[ph, "max_done"], b.count(2, 2))
                        need(pool, S[ph, "shift_ps"], b.count(1, -1))
                        nc.gpsimd.tensor_tensor(shift[q][:, :, 0, :], smax[q][:, :, :],
                                                zeros[:, 0:H].rearrange("n (a p) -> n a p", a=2), ALU.add).then_inc(S[ph, "shift_hi"], 1)
                        pool.wait_ge(S[ph, "shift_hi"], b.count(1, 1))
                        nc.gpsimd.tensor_tensor(shift[q][:, :, 1, :], smax[q][:, :, :], shift[q][:, :, 0, :],
                                                ALU.subtract).then_inc(S[ph, "shift_done"], 1)

                steps(pool, step)

            for ph in (SELF, CROSS):
                root(ph)
                groups(pool, lambda g: project(ph, g))
                attend(ph)
            root(FFN)

            def expert(b):
                pool.wait_ge(f_acc, b.count(8, 8))
                nc.gpsimd.tensor_tensor(result[:, b.count(), :], acc[b.slot(2)][0][:, :], acc[b.slot(2)][1][:, :],
                                        ALU.add).then_inc(f_result, 1)

            tiles(pool, lambda g: None, expert)


NAMES = ["x", "ctx_1024", "L0_attn_Wq", "L0_attn_Wk", "L0_attn_Wv", "L0_xattn_Wq", "L0_xattn_bq", "L0_xattn_Wk",
         "L0_xattn_bk", "L0_xattn_Wv", "L0_xattn_bv", "L0_xattn_Wo", "L0_xattn_bo", "L0_ffn_router_w",
         "L0_ffn_expert_weights"]


def shape_constants():
    ident = np.eye(C, dtype=np.float32)
    order, rotate = np.zeros((C, C), np.float32), np.zeros((C, C), np.float32)
    cosines, sines = np.zeros((C, N), np.float32), np.zeros((C, N), np.float32)
    inv = np.power(np.float32(10000.0), (np.float32(-2.0) * np.arange(D // 2, dtype=np.float32) / np.float32(D)), dtype=np.float32)
    angle = np.arange(N, dtype=np.float32)[:, None] * inv[None, :]
    for a in range(2):
        for d in range(D):
            for p in range(HALF):
                row = a * 64 + d * HALF + p
                channel = (a * HALF + p) * D + d
                order[channel, row] = 1.0
                if d % 2 == 0:
                    rotate[channel + 1, row] = -1.0
                else:
                    rotate[channel - 1, row] = 1.0
                cosines[row], sines[row] = np.cos(angle[:, d // 2]), np.sin(angle[:, d // 2])
    return {"ident": ident, "order": order, "rotate": rotate, "cosines": cosines, "sines": sines}


def kernel(**inputs):
    import concourse.bacc as bacc
    from concourse.bass_utils import run_bass_kernel_spmd as run

    nc = bacc.Bacc("TRN2", target_bir_lowering=False, num_devices=1)
    arrays, args = {}, []
    for name, a in [(n, np.ascontiguousarray(inputs[n])) for n in NAMES] + list(shape_constants().items()):
        arrays[f"in_{name}"] = a
        args.append(nc.dram_tensor(f"in_{name}", a.shape, mybir.dt.from_np(a.dtype), kind="ExternalInput").ap())
    args.append(nc.dram_tensor("out", (B, N, C), F32, kind="ExternalOutput").ap())
    build(nc, *args)
    r = run(nc, [arrays], core_ids=[0])
    return r.results[0]["out"]
```

```python
from contextlib import ExitStack

import numpy as np

import concourse.bass as bass
from concourse import mybir
from concourse.alu_op_type import AluOpType as ALU

ACT = mybir.ActivationFunctionType
AX = mybir.AxisListType
F32 = mybir.dt.float32
BF16 = mybir.dt.bfloat16

B, N, C = 16, 128, 128
H, D = 16, 8
E = 8
GB = 4
NG = B // GB
TW = GB * N
HALF = H // 2
TERMS = 6
SLOTS = 8
ROWS = TERMS * D
SHIFT_ROWS = slice(ROWS, ROWS + 4)
STORED = B * N // 2
SELF, CROSS, FFN = "self", "cross", "ffn"
LINKS = 14
EPS = 1e-5


class Step:

    def __init__(self, i, c, per=4):
        self.i, self.c, self.per = i, c, per

    def __add__(self, k):
        return Step(self.i, self.c + k, self.per)

    def count(self, per=1, more=0):
        static = per * self.c + more
        return static if self.i is None else self.i * (per * self.per) + static

    def turn(self, per=1, more=0):
        static = per * (self.c // 4) + more
        return static if self.i is None else self.i * per + static

    def slot(self, n):
        return self.c % n


def build(nc, x, ctx_in, wq1, wk1, wv1, wq2, bq2, wk2, bk2, wv2, bv2, wo2, bo2, router, experts,
          ident, order, rotate, cosines, sines, out):
    with ExitStack() as stack:
        def sb(name, shape, dt=F32):
            return stack.enter_context(nc.sbuf_tensor(name, shape, dt))

        def sem(name):
            return stack.enter_context(nc.semaphore(name))

        ps01 = stack.enter_context(nc.psum_tensor("ps01", [128, 2, 512], F32))
        ps23 = stack.enter_context(nc.psum_tensor("ps23", [128, 2, 512], F32))
        ps4 = stack.enter_context(nc.psum_tensor("ps4", [128, 512], F32))
        ps5 = stack.enter_context(nc.psum_tensor("ps5", [128, 512], F32))
        ps6 = stack.enter_context(nc.psum_tensor("ps6", [128, 512], F32))
        ps7 = stack.enter_context(nc.psum_tensor("ps7", [128, 512], F32))

        ident_s, order_s, rotate_s = sb("ident_s", [128, 128]), sb("order_s", [128, 128]), sb("rotate_s", [128, 128])
        ident_b = sb("ident_b", [128, 128], BF16)
        cos_s, sin_s = sb("cos_s", [128, N]), sb("sin_s", [128, N])
        raw = sb("raw", [128, 7, 128])
        wt = sb("wt", [128, 9, 128])
        Q1, RQ1, K1, RK1, V1, Q2, K2, V2, O2 = range(9)
        bqk_raw, bqk = sb("bqk_raw", [128, 2]), sb("bqk", [128, 2])
        brow = sb("brow", [1, 2, 128])
        bvo = sb("bvo", [128, 2, 128])
        ones_row = sb("ones_row", [1, 128])
        router_raw, router_t = sb("router_raw", [E, 128]), sb("router_t", [128, E])
        experts_s = sb("experts_s", [128, E, 128])
        zero_rows = sb("zero_rows", [128, B * N], BF16)
        minus_ones = sb("minus_ones", [2, 4 * HALF * N], BF16)
        before = sb("before", [128, E, E])
        minus_half = sb("minus_half", [128, B])
        zeros = sb("zeros", [128, HALF * D])

        hid = sb("hid", [128, B, C])
        context = sb("context", [128, B, C])
        stats = sb("stats", [128, B, 6])
        mean, rstd = sb("mean", [128, B]), sb("rstd", [128, B])
        ln_a, ln_b, ln_c, ln_d, ln_e, ln_f = (sb(f"ln_{n}", [128, B]) for n in "abcdef")
        xh = sb("xh", [128, GB, C])
        cg = sb("cg", [128, GB, C])
        xt, ct = sb("xt", [128, TW]), sb("ct", [128, TW])
        rope_a = [sb(f"rope_a{o}", [128, TW]) for o in range(2)]
        rope_b = [sb(f"rope_b{o}", [128, TW]) for o in range(2)]
        full = [sb(f"full{o}", [128, TW]) for o in range(2)]
        rest = [sb(f"rest{o}", [128, TW]) for o in range(2)]
        part = [sb(f"part{o}", [128, 3, B * N], BF16) for o in range(2)]
        vall = sb("vall", [128, B, C])
        qst = [sb(f"qst{q}", [128, HALF, N], BF16) for q in range(4)]
        kst = sb("kst", [128, 4, 2, HALF, N], BF16)
        smax = [sb(f"smax{q}", [128, 2, HALF]) for q in range(2)]
        shift = [sb(f"shift{q}", [128, 2, 2, HALF], BF16) for q in range(2)]
        shift_t = [sb(f"shift_t{q}", [4 * HALF, N], BF16) for q in range(2)]
        probs = [sb(f"probs{q}", [128, 2, 2, 4, N]) for q in range(2)]
        vpad = [sb(f"vpad{q}", [128, HALF, 2, 32]) for q in range(2)]
        ot = [sb(f"ot{q}", [128, 2, N]) for q in range(2)]
        rsum = [sb(f"rsum{q}", [128, H]) for q in range(2)]
        att = [sb(f"att{q}", [128, H, D]) for q in range(2)]
        att_t = [sb(f"att_t{q}", [128, N]) for q in range(2)]
        xt_all = sb("xt_all", [128, B, N])
        gate = sb("gate", [128, B, E])
        gbias = sb("gbias", [128, B])
        g_l, g_p, g_w, g_q, g_r = (sb(f"g_{n}", [128, GB, E]) for n in "lpwqr")
        g_gt, g_eq, g_lo = (sb(f"g_{n}", [128, GB, E, E]) for n in ("gt", "eq", "lo"))
        g_s = sb("g_s", [128, 6, GB])
        xe = [sb(f"xe{q}", [128, N]) for q in range(2)]
        acc = [[sb(f"acc{q}{h}", [128, C]) for h in range(2)] for q in range(2)]
        result = sb("result", [128, B, C])

        scratch = [nc.dram_tensor(f"scratch{o}", [2, SLOTS, 64, B * N], BF16).ap() for o in range(2)]

        const_in, weights_in, x_in, ctx_in_done, experts_in = (
            sem(n) for n in ("const_in", "weights_in", "x_in", "ctx_in_done", "experts_in"))
        pool_const, dve_const, kst_zero, w_ps, w_sb, fill_out = (
            sem(n) for n in ("pool_const", "dve_const", "kst_zero", "w_ps", "w_sb", "fill_out"))
        x_stats = sem("x_stats")
        ln_step = {k: sem(f"ln_step_{k}") for k in (SELF, CROSS, FFN)}
        rstd_done = {k: sem(f"rstd_done_{k}") for k in (SELF, CROSS, FFN)}
        PROJECT = ("xh_done",
                   "x_ps",
                   "x_sb",
                   "proj",
                   "q_read", "k_read",
                   "q_full", "k_full",
                   "part1", "rest", "part2", "part3",
                   "v_sb")
        ATTEND = ("s_ps", "max_done",
                  "shift_hi", "shift_done", "shift_ps", "shift_sb",
                  "r_ps", "exp_done",
                  "vpad_done", "pv",
                  "ot_sb", "ot_ps",
                  "rsum_done", "att_done",
                  "att_ps", "att_sb", "y_ps", "bias_done",
                  "hid_done", "stat_done")
        S = {(ph, n): sem(f"{ph}_{n}") for ph in (SELF, CROSS) for n in PROJECT + ATTEND}
        parts_out = {(ph, r): sem(f"{ph}_parts_out{r}") for ph in (SELF, CROSS) for r in range(2)}
        stack_in = {(ph, q): sem(f"{ph}_stack_in{q}") for ph in (SELF, CROSS) for q in range(4)}
        shift_in = {(ph, q): sem(f"{ph}_shift_in{q}") for ph in (SELF, CROSS) for q in range(4)}
        (f_xh, f_xps, f_xsb, f_logits, f_logits_read, f_exp, f_link, f_gate,
         f_xe, f_y, f_acc, f_result, f_out) = (
            sem(f"ffn_{n}") for n in ("xh", "x_ps", "x_sb", "logits", "logits_read", "exp", "link", "gate",
                                      "xe", "y", "acc", "result", "out"))

        def need(eng, s, value):
            if not (isinstance(value, int) and value <= 0):
                eng.wait_ge(s, value)

        def groups(eng, body):
            body(Step(None, 0, 1), True)
            with eng.Fori(1, NG - 1) as i:
                body(Step(i, 0, 1), True)
            body(Step(None, NG - 1, 1), False)

        def steps(eng, body):
            for c in range(-2, GB):
                body(Step(None, c))
            with eng.Fori(1, NG - 1) as i:
                for c in range(GB):
                    body(Step(i, c))
            for c in range(B - GB, B + 4):
                body(Step(None, c))

        def tiles(eng, front, expert):
            front(Step(None, 0, 1))
            front(Step(None, 1, 1))
            for c in range(GB):
                expert(Step(None, c))
            with eng.Fori(1, NG - 1) as i:
                front(Step(i, 1, 1))
                for c in range(GB):
                    expert(Step(i, c))
            for c in range(B - GB, B):
                expert(Step(None, c))

        def live(b):
            return b.i is not None or 0 <= b.c < B

        def of_group(t, g):
            return t[:, bass.ds(g.count(GB), GB)]

        def batches(ap):
            return ap.rearrange("p (b n) -> p b n", b=GB)

        def part_of(o, n, g):
            return part[o][:, n, bass.ds(g.count(TW), TW)]

        block = stack.enter_context(nc.Block())

        @block.sync
        def _(sp):
            for dst, src in ((ident_s, ident), (order_s, order), (rotate_s, rotate), (cos_s, cosines), (sin_s, sines)):
                sp.dma_start(dst[:, :], src).then_inc(const_in, 16)
            for n, w in enumerate((wq1, wk1, wv1, wq2, wk2, wv2, wo2)):
                sp.dma_start(raw[:, n, :], w).then_inc(weights_in, 16)
            for n, v in enumerate((bq2, bk2)):
                sp.dma_start(bqk_raw[:, n:n + 1], v.rearrange("(c a) -> c a", a=1)).then_inc(weights_in, 16)
            for n, v in enumerate((bv2, bo2)):
                sp.dma_start(brow[:, n, :], v.rearrange("(a c) -> a c", a=1)).then_inc(weights_in, 16)
            sp.dma_start(router_raw[:, :], router).then_inc(weights_in, 16)
            sp.dma_start(context[:, :, :], ctx_in.rearrange("b n c -> n b c")).then_inc(ctx_in_done, 16)
            sp.dma_start(experts_s[:, :, :], experts.rearrange("e h o -> h e o")).then_inc(experts_in, 16)
            sp.wait_ge(pool_const, 1)
            for a in range(2):
                sp.dma_start(scratch[0][a, TERMS:SLOTS].rearrange("t c n -> (t c) n"), zero_rows[:, :]).then_inc(fill_out, 16)
            sp.wait_ge(kst_zero, 1)
            for a in range(2):
                sp.dma_start(kst[ROWS + 2 * a:ROWS + 2 * a + 2, :, a, :, :].rearrange("r q p n -> r q (p n)"),
                             minus_ones[:, :].rearrange("r (q c) -> r q c", q=4)).then_inc(fill_out, 16)

            def store_parts(ph, r):
                tokens = slice(r * STORED, (r + 1) * STORED)
                for o in range(2):
                    sp.wait_ge(S[ph, "part2"], NG * r + NG - 1 + o)
                    sp.wait_ge(S[ph, "part3"], NG * r + NG - 1 + o)
                    for n, (first, count) in enumerate(((0, 3), (3, 2), (5, 1))):
                        src = part[0][:, 0:count, tokens] if o == 0 else part[1][:, n:n + 1, tokens].broadcast_to(
                            [128, count, STORED])
                        for a in range(2):
                            sp.dma_start(scratch[o][a, first:first + count, :, tokens].rearrange("t c n -> c t n"),
                                         src[64 * a:64 * a + 64]).then_inc(parts_out[ph, r], 16)

            def attend(ph):
                def load(b):
                    q = b.slot(4)
                    token = bass.ds(b.count(N), N)
                    sp.dma_start(qst[q][:, :, :], scratch[0].rearrange("a t (d p) n -> (a t d) p n", d=D)[:, :, token]).then_inc(
                        stack_in[ph, q], 16)
                    for a in range(2):
                        src = scratch[1][a, 0:TERMS].rearrange("t (d p) n -> (t d) p n", d=D)
                        sp.dma_start(kst[64 * a:64 * a + ROWS, q, a, :, :], src[:, :, token]).then_inc(stack_in[ph, q], 16)

                sp.wait_ge(parts_out[ph, 0], 16 * 4 * 3)
                if ph == SELF:
                    sp.wait_ge(fill_out, 16 * 4)
                for c in range(4):
                    load(Step(None, c))
                store_parts(ph, 1)
                sp.wait_ge(parts_out[ph, 1], 16 * 4 * 3)

                def step(t):
                    b = t + 1
                    if live(b):
                        sp.wait_ge(S[ph, "shift_sb"], b.count(1, 1))
                        sp.dma_start(qst[b.slot(4)][SHIFT_ROWS, :, :], shift_t[b.slot(2)][:, :]).then_inc(
                            shift_in[ph, b.slot(4)], 16)
                    if live(t) and live(t + 4):
                        sp.wait_ge(S[ph, "r_ps"], t.count(2, 2))
                        load(t + 4)

                steps(sp, step)

            for ph in (SELF, CROSS):
                store_parts(ph, 0)
                attend(ph)

            for g in range(NG):
                own = slice(GB * g, GB * (g + 1))
                sp.wait_ge(f_result, GB * (g + 1))
                sp.dma_start(out[own].rearrange("b n c -> n b c"), result[:, own, :]).then_inc(f_out, 16)
            sp.wait_ge(f_out, 16 * NG)

        @block.tensor
        def _(pe):
            pe.wait_ge(const_in, 16 * 5)
            pe.wait_ge(weights_in, 16 * 12)
            pe.wait_ge(dve_const, 2)
            plan = ((Q1, 0, order_s), (RQ1, 0, rotate_s), (K1, 1, order_s), (RK1, 1, rotate_s), (V1, 2, ident_s),
                    (Q2, 3, order_s), (K2, 4, order_s), (V2, 5, ident_s), (O2, 6, ident_s))
            for n, src, turn in plan:
                dst = (ps01[:, 0], ps01[:, 1], ps23[:, 0])[n // 4]
                pe.matmul(dst[:, 128 * (n % 4):128 * (n % 4) + 128], raw[:, src, :], turn[:, :], start=True, stop=True)
            pe.matmul(ps4[:, 0:2], order_s[:, :], bqk_raw[:, :], start=True, stop=True)
            pe.matmul(ps4[:, 8:8 + E], router_raw[:, :], ident_s[0:E, 0:E], start=True, stop=True)
            pe.matmul(ps4[:, 128:384], ones_row[:, :], brow[:, :, :].rearrange("a b c -> a (b c)"),
                      start=True, stop=True).then_inc(w_ps, 1)
            pe.wait_ge(w_sb, 1)

            def turn(ph, g):
                pe.wait_ge(S[ph, "xh_done"], g.count(1, 1))
                need(pe, S[ph, "x_sb"], g.count(1))
                for j in range(GB):
                    last = pe.transpose(ps5[:, N * j:N * j + N], xh[:, j, :], ident_s[:, :])
                    if ph == CROSS:
                        last = pe.transpose(ps6[:, N * j:N * j + N], cg[:, j, :], ident_s[:, :])
                last.then_inc(S[ph, "x_ps"], 1)

            def project(ph, g, more):
                w_q, w_k, w_v = (Q1, K1, V1) if ph == SELF else (Q2, K2, V2)
                src = xt if ph == SELF else ct
                pe.wait_ge(S[ph, "x_sb"], g.count(1, 1))
                need(pe, S[ph, "q_read"], g.count(1))
                last = pe.matmul(ps01[:, 0], wt[:, w_q, :], xt[:, :], start=True, stop=True)
                if ph == SELF:
                    last = pe.matmul(ps01[:, 1], wt[:, RQ1, :], xt[:, :], start=True, stop=True)
                last.then_inc(S[ph, "proj"], 1)
                need(pe, S[ph, "k_read"], g.count(1))
                last = pe.matmul(ps23[:, 0], wt[:, w_k, :], src[:, :], start=True, stop=True)
                if ph == SELF:
                    last = pe.matmul(ps23[:, 1], wt[:, RK1, :], src[:, :], start=True, stop=True)
                last.then_inc(S[ph, "proj"], 1)
                need(pe, S[ph, "v_sb"], g.count(1))
                for j in range(GB):
                    last = pe.matmul(ps4[:, C * j:C * j + C], src[:, N * j:N * j + N], wt[:, w_v, :], start=True, stop=True)
                last.then_inc(S[ph, "proj"], 1)
                if more:
                    turn(ph, g + 1)

            def attend(ph):
                for read in ("q_read", "k_read", "v_sb"):
                    pe.wait_ge(S[ph, read], NG)

                def scores(b, u):
                    q = b.slot(4)
                    if u == 0:
                        pe.wait_ge(stack_in[ph, q], b.turn(48, 48))
                    need(pe, S[ph, "max_done"], b.count(2, u))
                    for p in range(4 * u, 4 * u + 4):
                        for a in range(2):
                            last = pe.matmul(ps01[:, a, N * (p % 4):N * (p % 4) + N], qst[q][:, p, :], kst[:, q, a, p, :],
                                             start=True, stop=True)
                    last.then_inc(S[ph, "s_ps"], 1)

                def shifted(b, u):
                    q = b.slot(4)
                    if u == 0:
                        pe.wait_ge(shift_in[ph, q], b.turn(16, 16))
                    need(pe, S[ph, "exp_done"], b.count(2, u))
                    for p in range(4 * u, 4 * u + 4):
                        for a in range(2):
                            last = pe.matmul(ps23[:, a, N * (p % 4):N * (p % 4) + N], kst[:, q, a, p, :], qst[q][:, p, :],
                                             start=True, stop=True)
                    last.then_inc(S[ph, "r_ps"], 1)

                def weigh(b, r):
                    if r == 0:
                        pe.wait_ge(S[ph, "exp_done"], b.count(2, 2))
                        pe.wait_ge(S[ph, "vpad_done"], b.count(1, 1))
                        need(pe, S[ph, "ot_sb"], b.count(1))
                    for s in range(2):
                        for j in range(4):
                            p = 2 * j + s
                            last = pe.matmul(ps4[32 * j:32 * j + 32, N * r:N * r + N], vpad[b.slot(2)][:, 4 * r + j, s, :],
                                             probs[b.slot(2)][:, p // 4, r, p % 4, :], start=(s == 0), stop=(s == 1),
                                             tile_position=(0, 32 * j))
                    if r == 1:
                        last.then_inc(S[ph, "pv"], 1)

                def step(t):
                    if live(t + 2):
                        scores(t + 2, 0)
                    b = t + -2
                    if live(b):
                        pe.wait_ge(S[ph, "ot_sb"], b.count(1, 1))
                        need(pe, S[ph, "att_done"], b.count(1))
                        for r in range(2):
                            last = pe.transpose(ps6[:, N * r:N * r + N], ot[b.slot(2)][:, r, :], ident_s[:, :])
                        last.then_inc(S[ph, "ot_ps"], 1)
                    b = t + -3
                    if ph == CROSS and live(b):
                        pe.wait_ge(S[ph, "att_done"], b.count(1, 1))
                        need(pe, S[ph, "hid_done"], b.count(1))
                        pe.transpose(ps7[:, 0:N], att[b.slot(2)][:, :, :].rearrange("n h d -> n (h d)"),
                                     ident_s[:, :]).then_inc(S[ph, "att_ps"], 1)
                    if live(t):
                        shifted(t, 0)
                    b = t + 1
                    if live(b):
                        pe.wait_ge(S[ph, "shift_done"], b.count(1, 1))
                        need(pe, S[ph, "shift_sb"], b.count(1))
                        pe.transpose(ps5[0:4 * HALF, 0:N // 2].bitcast(BF16),
                                     shift[b.slot(2)][:, :, :, :].rearrange("n a s p -> n (a s p)"),
                                     ident_b[:, :]).then_inc(S[ph, "shift_ps"], 1)
                    if live(t + -1):
                        weigh(t + -1, 0)
                    if live(t + 2):
                        scores(t + 2, 1)
                    if live(t):
                        shifted(t, 1)
                    b = t + -3
                    if ph == CROSS and live(b):
                        pe.wait_ge(S[ph, "att_sb"], b.count(1, 1))
                        pe.matmul(ps7[:, N:N + C], att_t[b.slot(2)][:, :], wt[:, O2, :], start=True,
                                  stop=True).then_inc(S[ph, "y_ps"], 1)
                    if live(t + -1):
                        weigh(t + -1, 1)

                steps(pe, step)

            for ph in (SELF, CROSS):
                turn(ph, Step(None, 0, 1))
                groups(pe, lambda g, more: project(ph, g, more))
                attend(ph)

            def front(g):
                pe.wait_ge(f_xh, g.count(1, 1))
                need(pe, f_xsb, g.count(1))
                for j in range(GB):
                    last = pe.transpose(ps5[:, N * j:N * j + N], xh[:, j, :], ident_s[:, :])
                last.then_inc(f_xps, 1)
                pe.wait_ge(f_xsb, g.count(1, 1))
                need(pe, f_logits_read, g.count(1))
                for j in range(GB):
                    last = pe.matmul(ps6[:, E * j:E * j + E], xt[:, N * j:N * j + N], router_t[:, :], start=True, stop=True)
                last.then_inc(f_logits, 1)

            def expert(b):
                y = (ps01, ps23)[b.slot(2)]
                pe.wait_ge(f_xe, b.count(1, 1))
                need(pe, f_acc, b.count(8, -8))
                for h in range(2):
                    last = pe.matmul(y[:, h], xe[b.slot(2)][:, :],
                                     experts_s[:, 4 * h:4 * h + 4, :].rearrange("h e o -> h (e o)"), start=True, stop=True)
                last.then_inc(f_y, 1)

            pe.wait_ge(experts_in, 16)
            tiles(pe, front, expert)

        @block.scalar
        def _(act):
            act.dma_start(hid[:, :, :], x.rearrange("b n c -> n b c")).then_inc(x_in, 16)
            act.wait_ge(w_ps, 1)
            for n in range(2):
                nc.scalar.copy(wt[:, 4 * n:4 * n + 4, :].rearrange("i n o -> i (n o)"), ps01[:, n])
            nc.scalar.copy(wt[:, 8, :], ps23[:, 0, 0:128])
            nc.scalar.copy(bqk[:, :], ps4[:, 0:2])
            nc.scalar.copy(router_t[:, :], ps4[:, 8:8 + E])
            nc.scalar.copy(bvo[:, :, :].rearrange("n a c -> n (a c)"), ps4[:, 128:384]).then_inc(w_sb, 1)
            act.wait_ge(w_sb, 1)

            def copy_inputs(ph, g):
                act.wait_ge(S[ph, "x_ps"], g.count(1, 1))
                need(act, S[ph, "proj"], g.count(3))
                last = nc.scalar.copy(xt[:, :], ps5[:, :])
                if ph == CROSS:
                    last = nc.scalar.copy(ct[:, :], ps6[:, :])
                last.then_inc(S[ph, "x_sb"], 1)

            def project(ph, g, more):
                for o, (read, whole) in enumerate((("q_read", "q_full"), ("k_read", "k_full"))):
                    if ph == CROSS:
                        act.wait_ge(S[ph, "proj"], g.count(3, o + 1))
                        need(act, S[ph, "rest"], g.count(2, o - 1))
                        nc.scalar.activation(full[o][:, :], (ps01, ps23)[o][:, 0], ACT.Identity,
                                             bias=bqk[:, o:o + 1]).then_inc(S[ph, read], 1)
                        act.wait_ge(S[ph, read], g.count(1, 1))
                    else:
                        act.wait_ge(S[ph, whole], g.count(1, 1))
                    nc.scalar.copy(part_of(o, 0, g), full[o][:, :]).then_inc(S[ph, "part1"], 1)
                    if ph == SELF and o == 0:
                        act.wait_ge(S[ph, "proj"], g.count(3, 3))
                        nc.scalar.copy(of_group(vall, g), batches(ps4[:, :])).then_inc(S[ph, "v_sb"], 1)
                        if more:
                            copy_inputs(ph, g + 1)
                if ph == CROSS and more:
                    copy_inputs(ph, g + 1)
                for o in range(2):
                    act.wait_ge(S[ph, "rest"], g.count(2, o + 1))
                    nc.scalar.copy(part_of(o, 1, g), rest[o][:, :]).then_inc(S[ph, "part2"], 1)

            def attend(ph):
                def exponentials(b, u):
                    act.wait_ge(S[ph, "r_ps"], b.count(2, u + 1))
                    if u == 0:
                        need(act, S[ph, "pv"], b.count(1, -1))
                    nc.scalar.activation(probs[b.slot(2)][:, u, :, :, :].rearrange("m a p n -> m (a p n)"),
                                         ps23[:, :, :].rearrange("m a n -> m (a n)"), ACT.Exp,
                                         scale=D ** -0.5).then_inc(S[ph, "exp_done"], 1)

                def step(t):
                    if live(t):
                        exponentials(t, 0)
                    b = t + 1
                    if live(b):
                        act.wait_ge(S[ph, "shift_ps"], b.count(1, 1))
                        old = b + -2
                        if live(old):
                            act.wait_ge(shift_in[ph, old.slot(4)], old.turn(16, 16))
                        nc.scalar.copy(shift_t[b.slot(2)][:, :], ps5[0:4 * HALF, 0:N // 2].bitcast(BF16)).then_inc(
                            S[ph, "shift_sb"], 1)
                    b = t + -3
                    if ph == CROSS and live(b):
                        act.wait_ge(S[ph, "att_ps"], b.count(1, 1))
                        need(act, S[ph, "y_ps"], b.count(1, -1))
                        nc.scalar.copy(att_t[b.slot(2)][:, :], ps7[:, 0:N]).then_inc(S[ph, "att_sb"], 1)
                    if live(t):
                        exponentials(t, 1)
                    b = t + -1
                    if live(b):
                        act.wait_ge(S[ph, "pv"], b.count(1, 1))
                        need(act, S[ph, "ot_ps"], b.count(1, -1))
                        nc.scalar.copy(ot[b.slot(2)][:, :, :].rearrange("c r n -> c (r n)"), ps4[:, 0:2 * N]).then_inc(
                            S[ph, "ot_sb"], 1)

                steps(act, step)

            for ph in (SELF, CROSS):
                copy_inputs(ph, Step(None, 0, 1))
                groups(act, lambda g, more: project(ph, g, more))
                attend(ph)

            def front(g):
                act.wait_ge(f_xps, g.count(1, 1))
                need(act, f_logits, g.count(1))
                nc.scalar.copy(xt[:, :], ps5[:, :])
                nc.scalar.copy(of_group(xt_all, g), batches(ps5[:, :])).then_inc(f_xsb, 1)
                act.wait_ge(f_logits_read, g.count(1, 1))
                nc.scalar.activation(g_p[:, :, :], g_l[:, :, :], ACT.Exp).then_inc(f_exp, 1)

            def expert(b):
                act.wait_ge(f_xsb, b.turn(1, 1))
                need(act, f_y, b.count(1, -1))
                nc.scalar.copy(xe[b.slot(2)][:, :], xt_all[:, b.count(), :]).then_inc(f_xe, 1)

            tiles(act, front, expert)

        @block.vector
        def _(dve):
            nc.vector.memset(ones_row[:, :], 1.0).then_inc(dve_const, 1)
            nc.vector.memset(kst[:, :, :, :, :], 0.0).then_inc(kst_zero, 1)
            dve.wait_ge(const_in, 16 * 5)
            nc.vector.tensor_copy(ident_b[:, :], ident_s[:, :]).then_inc(dve_const, 1)
            dve.wait_ge(x_in, 16)
            for b in range(B):
                nc.vector.bn_stats(stats[:, b, :], hid[:, b, :]).then_inc(x_stats, 1)

            def layernorm(done, k):
                ln = ln_step[k]
                dve.wait_ge(done, B)
                nc.vector.tensor_tensor(ln_a[:, :], stats[:, :, 1], stats[:, :, 4], ALU.add).then_inc(ln, 1)
                nc.vector.tensor_tensor(ln_b[:, :], stats[:, :, 1], stats[:, :, 4], ALU.subtract).then_inc(ln, 1)
                nc.vector.tensor_tensor(ln_c[:, :], stats[:, :, 2], stats[:, :, 5], ALU.add).then_inc(ln, 1)
                dve.wait_ge(ln, 3)
                nc.vector.tensor_scalar(mean[:, :], ln_a[:, :], 0.5, None, ALU.mult).then_inc(ln, 1)
                nc.vector.scalar_tensor_tensor(ln_d[:, :], ln_b[:, :], 0.25, ln_b[:, :], ALU.mult, ALU.mult).then_inc(ln, 1)
                dve.wait_ge(ln, 5)
                nc.vector.scalar_tensor_tensor(ln_e[:, :], ln_c[:, :], 1.0 / C, ln_d[:, :], ALU.mult, ALU.add).then_inc(ln, 1)
                dve.wait_ge(ln, 6)
                nc.vector.tensor_scalar(ln_f[:, :], ln_e[:, :], EPS, None, ALU.add).then_inc(ln, 1)

            def normalise(g, k, last_read, done):
                dve.wait_ge(rstd_done[k], g.count(1, 1))
                need(dve, last_read, g.count(1))
                for j in range(GB):
                    b = g.count(GB, j)
                    last = nc.vector.tensor_scalar(xh[:, j, :], hid[:, b, :], mean[:, bass.ds(b, 1)], rstd[:, bass.ds(b, 1)],
                                                   ALU.subtract, ALU.mult)
                if done is not None:
                    last.then_inc(done, 1)

            def inputs(ph, g):
                normalise(g, ph, S[ph, "x_ps"], S[ph, "xh_done"] if ph == SELF else None)
                if ph == CROSS:
                    nc.vector.tensor_copy(cg[:, :, :], of_group(context, g)).then_inc(S[ph, "xh_done"], 1)

            def project(ph, g, more):
                if more:
                    inputs(ph, g + 1)
                if ph == CROSS:
                    dve.wait_ge(S[ph, "proj"], g.count(3, 3))
                    nc.vector.tensor_tensor(of_group(vall, g), batches(ps4[:, :]), bvo[:, 0:1, :].broadcast_to([128, GB, C]),
                                            ALU.add).then_inc(S[ph, "v_sb"], 1)
                    return
                cos_g = cos_s[:, :].unsqueeze(1).broadcast_to([128, GB, N])
                sin_g = sin_s[:, :].unsqueeze(1).broadcast_to([128, GB, N])
                for o, (ps, read, whole) in enumerate(((ps01, "q_read", "q_full"), (ps23, "k_read", "k_full"))):
                    dve.wait_ge(S[ph, "proj"], g.count(3, o + 1))
                    need(dve, S[ph, whole], g.count(1))
                    nc.vector.tensor_tensor(batches(rope_a[o][:, :]), batches(ps[:, 0]), cos_g, ALU.mult)
                    nc.vector.tensor_tensor(batches(rope_b[o][:, :]), batches(ps[:, 1]), sin_g, ALU.mult).then_inc(S[ph, read], 1)
                    dve.wait_ge(S[ph, read], g.count(1, 1))
                    need(dve, S[ph, "rest"], g.count(2, o - 1))
                    nc.vector.tensor_tensor(full[o][:, :], rope_a[o][:, :], rope_b[o][:, :], ALU.add).then_inc(S[ph, whole], 1)

            def attend(ph):
                def maxima(b, u):
                    dve.wait_ge(S[ph, "s_ps"], b.count(2, u + 1))
                    if u == 0:
                        need(dve, S[ph, "shift_done"], b.count(1, -1))
                    nc.vector.tensor_reduce(smax[b.slot(2)][:, :, 4 * u:4 * u + 4],
                                            ps01[:, :, :].rearrange("n a (p m) -> n a p m", p=4), AX.X,
                                            ALU.max).then_inc(S[ph, "max_done"], 1)

                def step(t):
                    if live(t + 2):
                        maxima(t + 2, 0)
                    b = t + -2
                    if live(b):
                        q = b.slot(2)
                        heads = ps6[:, 0:2 * N].rearrange("n (h e) -> n h e", h=H)
                        dve.wait_ge(S[ph, "ot_ps"], b.count(1, 1))
                        nc.vector.reciprocal(rsum[q][:, :].unsqueeze(2), heads[:, :, D:D + 1]).then_inc(S[ph, "rsum_done"], 1)
                        dve.wait_ge(S[ph, "rsum_done"], b.count(1, 1))
                        need(dve, S[ph, "hid_done" if ph == SELF else "att_ps"], b.count(1, -1))
                        nc.vector.tensor_tensor(att[q][:, :, :], heads[:, :, 0:D],
                                                rsum[q][:, :].unsqueeze(2).broadcast_to([128, H, D]),
                                                ALU.mult).then_inc(S[ph, "att_done"], 1)
                    if live(t + 2):
                        maxima(t + 2, 1)
                    b = t + -3
                    if ph == CROSS and live(b):
                        dve.wait_ge(S[ph, "y_ps"], b.count(1, 1))
                        dve.wait_ge(S[ph, "bias_done"], b.count(1, 1))
                        nc.vector.tensor_tensor(hid[:, b.count(), :], ps7[:, N:N + C], hid[:, b.count(), :],
                                                ALU.add).then_inc(S[ph, "hid_done"], 1)
                    b = t + (-3 if ph == SELF else -4)
                    if live(b):
                        dve.wait_ge(S[ph, "hid_done"], b.count(1, 1))
                        nc.vector.bn_stats(stats[:, b.count(), :], hid[:, b.count(), :]).then_inc(S[ph, "stat_done"], 1)

                steps(dve, step)

            layernorm(x_stats, SELF)
            inputs(SELF, Step(None, 0, 1))
            groups(dve, lambda g, more: project(SELF, g, more))
            attend(SELF)
            layernorm(S[SELF, "stat_done"], CROSS)
            dve.wait_ge(ctx_in_done, 16)
            inputs(CROSS, Step(None, 0, 1))
            groups(dve, lambda g, more: project(CROSS, g, more))
            attend(CROSS)
            layernorm(S[CROSS, "stat_done"], FFN)
            dve.wait_ge(pool_const, 3)

            def front(g):
                links = []

                def link(ins):
                    links.append(ins)
                    ins.then_inc(f_link, 1)
                    dve.wait_ge(f_link, g.count(LINKS, len(links)))

                logits = ps6[:, 0:GB * E].rearrange("n (b e) -> n b e", b=GB)
                per_tile = lambda k: g_s[:, k, :].unsqueeze(2).broadcast_to([128, GB, E])
                other = g_q[:, :, :].unsqueeze(2).broadcast_to([128, GB, E, E])
                mine = g_q[:, :, :].unsqueeze(3).broadcast_to([128, GB, E, E])
                normalise(g, FFN, f_xps, f_xh)
                dve.wait_ge(f_logits, g.count(1, 1))
                link(nc.vector.tensor_reduce(g_s[:, 0, :], logits, AX.X, ALU.max))
                nc.vector.tensor_tensor(g_l[:, :, :], logits, per_tile(0), ALU.subtract).then_inc(f_logits_read, 1)
                dve.wait_ge(f_exp, g.count(1, 1))
                link(nc.vector.tensor_reduce(g_s[:, 1, :], g_p[:, :, :], AX.X, ALU.add))
                link(nc.vector.reciprocal(g_s[:, 2, :], g_s[:, 1, :]))
                link(nc.vector.tensor_tensor(g_q[:, :, :], g_p[:, :, :], per_tile(2), ALU.mult))
                nc.vector.tensor_tensor(g_gt[:, :, :, :], other, mine, ALU.is_gt)
                link(nc.vector.tensor_tensor(g_eq[:, :, :, :], other, mine, ALU.is_equal))
                link(nc.vector.tensor_tensor(g_lo[:, :, :, :], g_eq[:, :, :, :],
                                             before[:, :, :].unsqueeze(1).broadcast_to([128, GB, E, E]), ALU.mult))
                link(nc.vector.tensor_tensor(g_eq[:, :, :, :], g_gt[:, :, :, :], g_lo[:, :, :, :], ALU.add))
                link(nc.vector.tensor_reduce(g_r[:, :, :], g_eq[:, :, :, :], AX.X, ALU.add))
                link(nc.vector.scalar_tensor_tensor(g_w[:, :, :], g_r[:, :, :], 1.5, g_q[:, :, :], ALU.is_lt, ALU.mult))
                link(nc.vector.tensor_reduce(g_s[:, 3, :], g_w[:, :, :], AX.X, ALU.add))
                link(nc.vector.tensor_scalar(g_s[:, 4, :], g_s[:, 3, :], 1e-6, None, ALU.add))
                link(nc.vector.reciprocal(g_s[:, 5, :], g_s[:, 4, :]))
                link(nc.vector.tensor_tensor(of_group(gate, g), g_w[:, :, :], per_tile(5), ALU.mult))
                link(nc.vector.tensor_tensor(g_r[:, :, :], of_group(gate, g), g_q[:, :, :], ALU.mult))
                nc.vector.tensor_reduce(of_group(gbias, g), g_r[:, :, :], AX.X, ALU.add).then_inc(f_gate, 1)
                assert len(links) == LINKS

            def expert(b):
                q, k = b.slot(2), b.count()
                dve.wait_ge(f_y, b.count(1, 1))
                dve.wait_ge(f_gate, b.turn(1, 1))
                need(dve, f_result, b.count(1, -1))
                for e in range(4):
                    for h in range(2):
                        y = (ps01, ps23)[q][:, h, C * e:C * e + C]
                        w = gate[:, k, 4 * h + e:4 * h + e + 1]
                        sums = acc[q][h]
                        if e:
                            dve.wait_ge(f_acc, b.count(8, 2 * e + h - 1))
                            ins = nc.vector.scalar_tensor_tensor(sums[:, :], y, w, sums[:, :], ALU.mult, ALU.add)
                        elif h == 0:
                            ins = nc.vector.scalar_tensor_tensor(sums[:, :], y, w, hid[:, k, :], ALU.mult, ALU.add)
                        else:
                            ins = nc.vector.tensor_scalar(sums[:, :], y, w, gbias[:, bass.ds(k, 1)], ALU.mult, ALU.add)
                        ins.then_inc(f_acc, 1)

            tiles(dve, front, expert)

        @block.gpsimd
        def _(pool):
            nc.gpsimd.memset(zeros[:, :], 0.0)
            nc.gpsimd.memset(minus_ones[:, :], -1.0)
            nc.gpsimd.memset(zero_rows[:, :], 0.0).then_inc(pool_const, 1)
            nc.gpsimd.memset(minus_half[:, :], -0.5)
            for q in range(2):
                nc.gpsimd.memset(vpad[q][:, :, :, :], 0.0)
            nc.gpsimd.memset(before[:, :, :], 0.0).then_inc(pool_const, 1)
            pool.wait_ge(pool_const, 2)
            for q in range(2):
                for s in range(2):
                    nc.gpsimd.memset(vpad[q][:, :, s, 2 * D * s + D:2 * D * s + 2 * D], 1.0)
            for e in range(1, E):
                last = nc.gpsimd.memset(before[:, e, 0:e], 1.0)
            last.then_inc(pool_const, 1)
            pool.wait_ge(pool_const, 3)

            def root(k):
                pool.wait_ge(ln_step[k], 7)
                for g in range(NG):
                    own = slice(GB * g, GB * (g + 1))
                    nc.gpsimd.tensor_tensor(rstd[:, own], ln_f[:, own], minus_half[:, own], ALU.pow).then_inc(rstd_done[k], 1)

            def project(ph, g):
                for o in range(2):
                    pool.wait_ge(S[ph, "part1"], g.count(2, o + 1))
                    need(pool, S[ph, "part2"], g.count(2, o - 1))
                    need(pool, S[ph, "part3"], g.count(2, o - 1))
                    nc.gpsimd.tensor_tensor(rest[o][:, :], full[o][:, :], part_of(o, 0, g), ALU.subtract).then_inc(S[ph, "rest"], 1)
                for o in range(2):
                    pool.wait_ge(S[ph, "part2"], g.count(2, o + 1))
                    pool.wait_ge(S[ph, "rest"], g.count(2, o + 1))
                    nc.gpsimd.tensor_tensor(part_of(o, 2, g), rest[o][:, :], part_of(o, 1, g), ALU.subtract).then_inc(S[ph, "part3"], 1)

            def attend(ph):
                pool.wait_ge(S[ph, "v_sb"], NG)
                pool.wait_ge(S[ph, "xh_done"], NG)

                def step(t):
                    b = t
                    if live(b):
                        need(pool, S[ph, "pv"], b.count(1, -1))
                        values = vall[:, b.count(), :].rearrange("m (j s d) -> m j s d", s=2, d=D)
                        for s in range(2):
                            last = nc.gpsimd.tensor_tensor(vpad[b.slot(2)][:, :, s, 2 * D * s:2 * D * s + D], values[:, :, s, :],
                                                           zeros[:, :].rearrange("n (j d) -> n j d", j=HALF), ALU.add)
                        last.then_inc(S[ph, "vpad_done"], 1)
                    b = t + -2
                    if live(b):
                        row = hid[:, b.count(), :]
                        if ph == SELF:
                            pool.wait_ge(S[ph, "att_done"], b.count(1, 1))
                            nc.gpsimd.tensor_tensor(row, att[b.slot(2)][:, :, :].rearrange("n h d -> n (h d)"), row,
                                                    ALU.add).then_inc(S[ph, "hid_done"], 1)
                        else:
                            nc.gpsimd.tensor_tensor(row, bvo[:, 1, :], row, ALU.add).then_inc(S[ph, "bias_done"], 1)
                    b = t + 2
                    if live(b):
                        q = b.slot(2)
                        pool.wait_ge(S[ph, "max_done"], b.count(2, 2))
                        need(pool, S[ph, "shift_ps"], b.count(1, -1))
                        nc.gpsimd.tensor_tensor(shift[q][:, :, 0, :], smax[q][:, :, :],
                                                zeros[:, 0:H].rearrange("n (a p) -> n a p", a=2), ALU.add).then_inc(S[ph, "shift_hi"], 1)
                        pool.wait_ge(S[ph, "shift_hi"], b.count(1, 1))
                        nc.gpsimd.tensor_tensor(shift[q][:, :, 1, :], smax[q][:, :, :], shift[q][:, :, 0, :],
                                                ALU.subtract).then_inc(S[ph, "shift_done"], 1)

                steps(pool, step)

            for ph in (SELF, CROSS):
                root(ph)
                groups(pool, lambda g, more: project(ph, g))
                attend(ph)
            root(FFN)

            def expert(b):
                pool.wait_ge(f_acc, b.count(8, 8))
                nc.gpsimd.tensor_tensor(result[:, b.count(), :], acc[b.slot(2)][0][:, :], acc[b.slot(2)][1][:, :],
                                        ALU.add).then_inc(f_result, 1)

            tiles(pool, lambda g: None, expert)


NAMES = ["x", "ctx_1024", "L0_attn_Wq", "L0_attn_Wk", "L0_attn_Wv", "L0_xattn_Wq", "L0_xattn_bq", "L0_xattn_Wk",
         "L0_xattn_bk", "L0_xattn_Wv", "L0_xattn_bv", "L0_xattn_Wo", "L0_xattn_bo", "L0_ffn_router_w",
         "L0_ffn_expert_weights"]


def shape_constants():
    ident = np.eye(C, dtype=np.float32)
    order, rotate = np.zeros((C, C), np.float32), np.zeros((C, C), np.float32)
    cosines, sines = np.zeros((C, N), np.float32), np.zeros((C, N), np.float32)
    inv = np.power(np.float32(10000.0), (np.float32(-2.0) * np.arange(D // 2, dtype=np.float32) / np.float32(D)), dtype=np.float32)
    angle = np.arange(N, dtype=np.float32)[:, None] * inv[None, :]
    for a in range(2):
        for d in range(D):
            for p in range(HALF):
                row = a * 64 + d * HALF + p
                channel = (a * HALF + p) * D + d
                order[channel, row] = 1.0
                if d % 2 == 0:
                    rotate[channel + 1, row] = -1.0
                else:
                    rotate[channel - 1, row] = 1.0
                cosines[row], sines[row] = np.cos(angle[:, d // 2]), np.sin(angle[:, d // 2])
    return {"ident": ident, "order": order, "rotate": rotate, "cosines": cosines, "sines": sines}


def kernel(**inputs):
    import concourse.bacc as bacc
    from concourse.bass_utils import run_bass_kernel_spmd as run

    nc = bacc.Bacc("TRN2", target_bir_lowering=False, num_devices=1)
    arrays, args = {}, []
    for name, a in [(n, np.ascontiguousarray(inputs[n])) for n in NAMES] + list(shape_constants().items()):
        arrays[f"in_{name}"] = a
        args.append(nc.dram_tensor(f"in_{name}", a.shape, mybir.dt.from_np(a.dtype), kind="ExternalInput").ap())
    args.append(nc.dram_tensor("out", (B, N, C), F32, kind="ExternalOutput").ap())
    build(nc, *args)
    r = run(nc, [arrays], core_ids=[0])
    return r.results[0]["out"]
```

```python
from contextlib import ExitStack

import numpy as np

import concourse.bass as bass
from concourse import mybir
from concourse.alu_op_type import AluOpType as ALU

ACT = mybir.ActivationFunctionType
AX = mybir.AxisListType
F32 = mybir.dt.float32
BF16 = mybir.dt.bfloat16

B, N, C = 16, 128, 128
H, D = 16, 8
E = 8
GB = 4
NG = B // GB
TW = GB * N
HALF = H // 2
TERMS = 6
ROWS = TERMS * 2 * D
DEPTH = ROWS + 4
SELF, CONTEXT, CROSS, FFN = "self", "context", "cross", "ffn"
Q, K, CONTEXT_K = range(3)
EPS = 1e-5


class Step:

    def __init__(self, i, c, per=4):
        self.i, self.c, self.per = i, c, per

    def __add__(self, k):
        return Step(self.i, self.c + k, self.per)

    def count(self, per=1, more=0):
        static = per * self.c + more
        return static if self.i is None else self.i * (per * self.per) + static

    def turn(self, per=1, more=0):
        static = per * (self.c // 4) + more
        return static if self.i is None else self.i * per + static

    def slot(self, n):
        return self.c % n

    def ring(self):
        group = self.c // 4
        return group % 2 if self.i is None else (self.i + group) % 2


def build(nc, x, ctx_in, wq1, wk1, wv1, wq2, bq2, wk2, bk2, wv2, bv2, wo2, bo2, router, experts,
          constants, out):
    with ExitStack() as stack:
        def sb(name, shape, dt=F32):
            return stack.enter_context(nc.sbuf_tensor(name, shape, dt))

        def sem(name):
            return stack.enter_context(nc.semaphore(name))

        ps01 = stack.enter_context(nc.psum_tensor("ps01", [128, 2, 512], F32))
        ps23 = stack.enter_context(nc.psum_tensor("ps23", [128, 2, 512], F32))
        ps4 = stack.enter_context(nc.psum_tensor("ps4", [128, 512], F32))
        ps5 = stack.enter_context(nc.psum_tensor("ps5", [128, 512], F32))
        ps6 = stack.enter_context(nc.psum_tensor("ps6", [128, 512], F32))
        ps7 = stack.enter_context(nc.psum_tensor("ps7", [128, 512], F32))

        constants_s = sb("constants_s", [128, 5, 128])
        ident_s, order_s, rotate_s, cos_s, sin_s = (constants_s[:, n, :] for n in range(5))
        ident_b = sb("ident_b", [128, 128], BF16)
        raw = sb("raw", [128, 7, 128])
        wt = sb("wt", [128, 9, 128])
        Q1, RQ1, K1, RK1, V1, Q2, K2, V2, O2 = range(9)
        bqk_raw, bqk = sb("bqk_raw", [128, 2]), sb("bqk", [128, 2])
        brow = sb("brow", [1, 2, 128])
        bvo = sb("bvo", [128, 2, 128])
        ones_row = sb("ones_row", [1, 128])
        router_raw, router_t = sb("router_raw", [E, 128]), sb("router_t", [128, E])
        experts_s = sb("experts_s", [128, E, 128])
        minus_ones = sb("minus_ones", [2, HALF * TW], BF16)
        falling = sb("falling", [128, E])
        minus_half = sb("minus_half", [128, B])
        zeros = sb("zeros", [128, HALF * D])

        hid = sb("hid", [128, B, C])
        context = sb("context", [128, B, C])
        stats = sb("stats", [128, B, 6])
        mean, rstd = sb("mean", [128, B]), sb("rstd", [128, B])
        ln_a, ln_b, ln_c, ln_d, ln_e, ln_f = (sb(f"ln_{n}", [128, B]) for n in "abcdef")
        xh = sb("xh", [128, GB, C])
        xg = sb("xg", [128, GB, C])
        xts = [sb(f"xt{q}", [128, TW]) for q in range(2)]
        xt = xts[0]
        rope_a = [sb(f"rope_a{o}", [128, TW]) for o in range(2)]
        rope_b = [sb(f"rope_b{o}", [128, TW]) for o in range(2)]
        full = [sb(f"full{o}", [128, TW]) for o in range(2)]
        rest = [sb(f"rest{o}", [128, TW]) for o in range(2)]
        part = [sb(f"part{o}", [128, 3, B * N], BF16) for o in (Q, K, CONTEXT_K)]
        vall = sb("vall", [128, B, C])
        qst = sb("qst", [128, 2, HALF, TW], BF16)
        kst = sb("kst", [128, 2, 2, HALF, TW], BF16)
        smax = [sb(f"smax{q}", [128, 2, HALF]) for q in range(2)]
        shift = [sb(f"shift{q}", [128, 2, 2, HALF], BF16) for q in range(2)]
        shift_t = [sb(f"shift_t{q}", [4 * HALF, N], BF16) for q in range(2)]
        probs = [sb(f"probs{q}", [128, 2, 2, 4, N]) for q in range(2)]
        vpad = [sb(f"vpad{q}", [128, HALF, 2, 32]) for q in range(2)]
        ot = [sb(f"ot{q}", [128, 2, N]) for q in range(2)]
        rsum = [sb(f"rsum{q}", [128, H]) for q in range(2)]
        att = [sb(f"att{q}", [128, H, D]) for q in range(2)]
        att_t = [sb(f"att_t{q}", [128, N]) for q in range(2)]
        xt_all = vall
        gate = sb("gate", [128, B, E])
        gbias = sb("gbias", [128, B])
        g_l, g_p, g_w, g_q, g_r = (sb(f"g_{n}", [128, B, E]) for n in "lpwqr")
        g_first = [sb(f"g_first{k}", [128, B, E]) for k in range(2)]
        g_s = sb("g_s", [128, 7, B])
        xe = [sb(f"xe{q}", [128, N]) for q in range(2)]
        term = [[sb(f"term{q}{h}", [128, C]) for h in range(2)] for q in range(2)]
        terms, sums = [sb(f"terms{q}", [128, C]) for q in range(2)], [sb(f"sums{q}", [128, C]) for q in range(2)]
        acc = [[sb(f"acc{q}{h}", [128, C]) for h in range(2)] for q in range(2)]

        scratch = [nc.dram_tensor(f"scratch{o}", [TERMS, 128, B * N], BF16).ap() for o in (Q, K, CONTEXT_K)]

        const_in, self_weights_in, weights_in, x_first, x_in, ctx_in_done, experts_in = (
            sem(n) for n in ("const_in", "self_weights_in", "weights_in", "x_first", "x_in", "ctx_in_done", "experts_in"))
        pool_const, dve_const, kst_zero, w_ps, w_sb, fill_out = (
            sem(n) for n in ("pool_const", "dve_const", "kst_zero", "w_ps", "w_sb", "fill_out"))
        x_stats = sem("x_stats")
        ln_step = {k: sem(f"ln_step_{k}") for k in (SELF, CROSS, FFN)}
        rstd_done = {k: sem(f"rstd_done_{k}") for k in (SELF, CROSS, FFN)}
        PROJECT = ("xh_done",
                   "x_ps",
                   "x_sb",
                   "proj",
                   "q_read", "k_read",
                   "q_full", "k_full",
                   "part1", "rest", "part2", "part3",
                   "v_sb")
        BIASED = ("xh_done", "x_ps", "x_sb", "proj",
                  "full",
                  "part1", "rest", "part2", "part3",
                  "v_sb")
        ATTEND = ("s_ps", "max_done",
                  "shift_hi", "shift_done", "shift_ps", "shift_sb",
                  "r_ps", "exp_done",
                  "vpad_done", "pv",
                  "ot_sb", "ot_ps",
                  "rsum_done", "att_done",
                  "att_ps", "att_sb", "y_ps", "bias_done",
                  "hid_done", "stat_done")
        S = {(ph, n): sem(f"{ph}_{n}") for ph, names in ((SELF, PROJECT + ATTEND), (CONTEXT, BIASED[1:]), (CROSS, BIASED[:-1] + ATTEND))
             for n in names}
        parts_out = {(ph, g): sem(f"{ph}_parts_out{g}")
                     for ph in (SELF, CONTEXT, CROSS) for g in range(NG)}
        stack_in = {(ph, j): sem(f"{ph}_stack_in{j}") for ph in (SELF, CROSS) for j in range(2)}
        shift_in = {(ph, q): sem(f"{ph}_shift_in{q}") for ph in (SELF, CROSS) for q in range(4)}
        (f_xh, f_xps, f_xsb, f_logits, f_exp, f_link, f_gate,
         f_xe, f_y, f_acc, f_term, f_terms, f_sums, f_result, f_out) = (
            sem(f"ffn_{n}") for n in ("xh", "x_ps", "x_sb", "logits", "exp", "link", "gate",
                                      "xe", "y", "acc", "term", "terms", "sums", "result", "out"))

        def need(eng, s, value):
            if not (isinstance(value, int) and value <= 0):
                eng.wait_ge(s, value)

        def groups(eng, body):
            body(Step(None, 0, 1), True)
            with eng.Fori(1, NG - 1) as i:
                body(Step(i, 0, 1), True)
            body(Step(None, NG - 1, 1), False)

        def steps(eng, body):
            for c in range(-2, GB):
                body(Step(None, c))
            with eng.Fori(1, NG - 1) as i:
                for c in range(GB):
                    body(Step(i, c))
            for c in range(B - GB, B + 4):
                body(Step(None, c))

        def tiles(eng, expert):
            for c in range(GB):
                expert(Step(None, c))
            with eng.Fori(1, NG - 1) as i:
                for c in range(GB):
                    expert(Step(i, c))
            for c in range(B - GB, B):
                expert(Step(None, c))

        def live(b):
            return b.i is not None or 0 <= b.c < B

        def of_group(t, g):
            return t[:, bass.ds(g.count(GB), GB)]

        def batches(ap):
            return ap.rearrange("p (b n) -> p b n", b=GB)

        def part_of(o, n, g):
            return part[o][:, n, bass.ds(g.count(TW), TW)]

        block = stack.enter_context(nc.Block())

        @block.sync
        def _(sp):
            sp.dma_start(constants_s[:, :, :], constants.rearrange("k r c -> r k c")).then_inc(const_in, 16)
            for n, w in enumerate((wq1, wk1, wv1, wq2, wk2, wv2, wo2)):
                sp.dma_start(raw[:, n, :], w).then_inc(self_weights_in if n < 3 else weights_in, 16)
            for n, v in enumerate((bq2, bk2)):
                sp.dma_start(bqk_raw[:, n:n + 1], v.rearrange("(c a) -> c a", a=1)).then_inc(weights_in, 16)
            for n, v in enumerate((bv2, bo2)):
                sp.dma_start(brow[:, n, :], v.rearrange("(a c) -> a c", a=1)).then_inc(weights_in, 16)
            sp.dma_start(router_raw[:, :], router).then_inc(weights_in, 16)
            sp.dma_start(context[:, :, :], ctx_in.rearrange("b n c -> n b c")).then_inc(ctx_in_done, 16)
            sp.dma_start(experts_s[:, :, :], experts.rearrange("e h o -> h e o")).then_inc(experts_in, 16)
            sp.wait_ge(pool_const, 1)
            sp.wait_ge(kst_zero, 3)
            for a in range(2):
                sp.dma_start(kst[ROWS + 2 * a:ROWS + 2 * a + 2, :, a, :, :].rearrange("r q p n -> r q (p n)"),
                             minus_ones[:, :].unsqueeze(1).broadcast_to([2, 2, HALF * TW])).then_inc(fill_out, 16)

            def store_parts(ph, o, g, count=1):
                tokens = slice(g * TW, (g + count) * TW)
                done = 2 * g + 1 + o if ph == SELF else g + count
                sp.wait_ge(S[ph, "part2"], done)
                sp.wait_ge(S[ph, "part3"], done)
                for n, (first, terms) in enumerate(((0, 3), (3, 2), (5, 1))):
                    src = part[Q][:, 0:terms, tokens] if o == Q else part[o][:, n:n + 1, tokens].broadcast_to(
                        [128, terms, count * TW])
                    sp.dma_start(scratch[o][first:first + terms, :, tokens].rearrange("t c n -> c t n"), src).then_inc(
                        parts_out[ph, g], 16)

            def places(b):
                return slice(b * N, (b + 2) * N), b // GB % 2, slice(b % GB * N, (b % GB + 2) * N)

            def load_q(ph, b):
                tokens, ring, own = places(b)
                sp.dma_start(qst[0:ROWS, ring, :, own],
                             scratch[Q].rearrange("t (r p) n -> (t r) p n", p=HALF)[:, :, tokens]).then_inc(
                    stack_in[ph, b % GB // 2], 16)

            def load_k(ph, b):
                tokens, ring, own = places(b)
                src = scratch[K if ph == SELF else CONTEXT_K].rearrange("t (d a p) n -> a (t d) p n", a=2, p=HALF)
                for a in range(2):
                    sp.dma_start(kst[a:ROWS:2, ring, a, :, own], src[a, :, :, tokens]).then_inc(stack_in[ph, b % GB // 2], 16)

            def attend(ph):
                for b in range(-1, B + 1):
                    if 0 <= b < B:
                        sp.wait_ge(S[ph, "shift_sb"], b + 1)
                        sp.dma_start(qst[ROWS:DEPTH, b // GB % 2, :, N * (b % GB):N * (b % GB) + N], shift_t[b % 2][:, :]).then_inc(
                            shift_in[ph, b % 4], 16)
                    if ph == SELF and b in (5, 7):
                        store_parts(CONTEXT, CONTEXT_K, b - 5, 2)
                    ahead = b + 4
                    if ahead >= GB and ahead % 2 == 0 and ahead < B:
                        if ahead % GB == 0:
                            sp.wait_ge(parts_out[ph, ahead // GB], 16 * (6 if ph == SELF else 3))
                        need(sp, S[ph, "r_ps"], 4 * (b - 2))
                        load_q(ph, ahead)
                        load_k(ph, ahead)

            for ph in (SELF, CROSS):
                own = (Q, K) if ph == SELF else (Q,)
                if ph == CROSS:
                    for g in (0, 2):
                        sp.wait_ge(parts_out[CONTEXT, g], 16 * 3)
                    sp.wait_ge(S[SELF, "r_ps"], 4 * B)
                    load_k(CROSS, 0)
                    load_k(CROSS, 2)
                for g in range(NG):
                    for o in own:
                        store_parts(ph, o, g)
                    if g == 1:
                        sp.wait_ge(parts_out[ph, 0], 16 * 3 * len(own))
                        if ph == SELF:
                            sp.wait_ge(fill_out, 16 * 2)
                        for b in (0, 2):
                            load_q(ph, b)
                            if ph == SELF:
                                load_k(ph, b)
                attend(ph)

            for g in range(NG):
                own = slice(GB * g, GB * (g + 1))
                sp.wait_ge(f_result, GB * (g + 1))
                sp.dma_start(out[own].rearrange("b n c -> n b c"), hid[:, own, :]).then_inc(f_out, 16)
            sp.wait_ge(f_out, 16 * NG)

        @block.tensor
        def _(pe):
            pe.wait_ge(const_in, 16)
            pe.wait_ge(self_weights_in, 16 * 3)
            for n, (src, order) in enumerate(((0, order_s), (0, rotate_s), (1, order_s), (1, rotate_s), (2, ident_s))):
                last = pe.matmul(ps01[:, n // 4, 128 * (n % 4):128 * (n % 4) + 128], raw[:, src, :], order, start=True, stop=True)
            last.then_inc(w_ps, 1)
            pe.wait_ge(w_sb, 1)

            def prepare_weights():
                pe.wait_ge(weights_in, 16 * 9)
                pe.wait_ge(dve_const, 2)
                for n, order in enumerate((order_s, order_s, ident_s, ident_s)):
                    pe.matmul(ps6[:, 128 * n:128 * n + 128], raw[:, 3 + n, :], order, start=True, stop=True)
                pe.matmul(ps7[:, 0:2], order_s, bqk_raw[:, :], start=True, stop=True)
                pe.matmul(ps7[:, 8:8 + E], router_raw[:, :], ident_s[0:E, 0:E], start=True, stop=True)
                pe.matmul(ps7[:, 128:384], ones_row[:, :], brow[:, :, :].rearrange("a b c -> a (b c)"),
                          start=True, stop=True).then_inc(w_ps, 1)

            def turn(ph, g):
                if ph == CONTEXT:
                    pe.wait_ge(ctx_in_done, 16)
                else:
                    pe.wait_ge(S[ph, "xh_done"], g.count(1, 1))
                need(pe, S[ph, "x_sb"], g.count(1))
                for j in range(GB):
                    last = pe.transpose(ps5[:, N * j:N * j + N],
                                        context[:, g.count(GB, j), :] if ph == CONTEXT else xh[:, j, :], ident_s)
                last.then_inc(S[ph, "x_ps"], 1)

            def values(ps, xt, w_v, signal):
                for j in range(GB):
                    last = pe.matmul(ps[:, C * j:C * j + C], xt[:, N * j:N * j + N], wt[:, w_v, :], start=True, stop=True)
                last.then_inc(signal, 1)

            def project_self(g, more):
                if not more:
                    prepare_weights()
                pe.wait_ge(S[SELF, "x_sb"], g.count(1, 1))
                for ps, read, w, w_rotated in ((ps01, "q_read", Q1, RQ1), (ps23, "k_read", K1, RK1)):
                    need(pe, S[SELF, read], g.count(1))
                    pe.matmul(ps[:, 0], wt[:, w, :], xt[:, :], start=True, stop=True)
                    pe.matmul(ps[:, 1], wt[:, w_rotated, :], xt[:, :], start=True, stop=True).then_inc(S[SELF, "proj"], 1)
                need(pe, S[SELF, "v_sb"], g.count(1))
                values(ps4, xt, V1, S[SELF, "proj"])
                turn(*((SELF, g + 1) if more else (CONTEXT, Step(None, 0, 1))))

            def project(ph, g):
                pe.wait_ge(S[ph, "x_sb"], g + 1)
                if ph == CONTEXT and g == 0:
                    pe.wait_ge(w_sb, 2)
                    pe.wait_ge(S[SELF, "k_read"], NG)
                    pe.wait_ge(S[SELF, "v_sb"], NG)
                need(pe, S[ph, "full"], g - 1)
                ps, weight = (ps01, Q2) if ph == CROSS else (ps23, K2)
                pe.matmul(ps[:, g % 2], wt[:, weight, :], xts[g % 2][:, :], start=True, stop=True).then_inc(S[ph, "proj"], 1)
                if ph == CONTEXT:
                    need(pe, S[CONTEXT, "v_sb"], g - 1)
                    values((ps4, ps6)[g % 2], xts[g % 2], V2, S[CONTEXT, "proj"])

            def attend(ph):
                for read in (((SELF, "q_read"), (CONTEXT, "full"), (CONTEXT, "v_sb")) if ph == SELF else
                             ((CROSS, "full"),)):
                    pe.wait_ge(S[read], NG)

                def scores(b, u, a):
                    q, own = b.ring(), slice(N * b.slot(4), N * b.slot(4) + N)
                    if u == 0 and a == 0:
                        if b.slot(2) == 0:
                            pe.wait_ge(stack_in[ph, b.slot(4) // 2], b.turn(48, 48))
                    need(pe, S[ph, "max_done"], b.count(4, 2 * u + a - 1))
                    for p in range(4 * u, 4 * u + 4):
                        last = pe.matmul(ps01[:, a, N * (p % 4):N * (p % 4) + N], qst[0:ROWS, q, p, own], kst[0:ROWS, q, a, p, own],
                                         start=True, stop=True)
                    last.then_inc(S[ph, "s_ps"], 1)

                def shifted(b, u, a):
                    q, own = b.ring(), slice(N * b.slot(4), N * b.slot(4) + N)
                    if u == 0 and a == 0:
                        pe.wait_ge(shift_in[ph, b.slot(4)], b.turn(16, 16))
                    need(pe, S[ph, "exp_done"], b.count(4, 2 * u + a - 1))
                    for p in range(4 * u, 4 * u + 4):
                        last = pe.matmul(ps23[:, a, N * (p % 4):N * (p % 4) + N], kst[0:DEPTH, q, a, p, own], qst[0:DEPTH, q, p, own],
                                         start=True, stop=True)
                    last.then_inc(S[ph, "r_ps"], 1)

                def weigh(b, r):
                    if r == 0:
                        pe.wait_ge(S[ph, "exp_done"], b.count(4, 4))
                        pe.wait_ge(S[ph, "vpad_done"], b.count(1, 1))
                        need(pe, S[ph, "ot_sb"], b.count(1))
                    for s in range(2):
                        for j in range(4):
                            p = 2 * j + s
                            last = pe.matmul(ps4[32 * j:32 * j + 32, N * r:N * r + N], vpad[b.slot(2)][:, 4 * r + j, s, :],
                                             probs[b.slot(2)][:, p // 4, r, p % 4, :], start=(s == 0), stop=(s == 1),
                                             tile_position=(0, 32 * j))
                    if r == 1:
                        last.then_inc(S[ph, "pv"], 1)

                def step(t):
                    if live(t + 2):
                        scores(t + 2, 0, 0)
                        scores(t + 2, 0, 1)
                    if live(t):
                        shifted(t, 0, 0)
                        shifted(t, 0, 1)
                    b = t + 1
                    if live(b):
                        pe.wait_ge(S[ph, "shift_done"], b.count(1, 1))
                        need(pe, S[ph, "shift_sb"], b.count(1))
                        pe.transpose(ps5[0:4 * HALF, 0:N // 2].bitcast(BF16),
                                     shift[b.slot(2)][:, :, :, :].rearrange("n a s p -> n (a s p)"),
                                     ident_b[:, :]).then_inc(S[ph, "shift_ps"], 1)
                    b = t + -2
                    if live(b):
                        pe.wait_ge(S[ph, "ot_sb"], b.count(1, 1))
                        need(pe, S[ph, "att_done"], b.count(1))
                        for r in range(2):
                            last = pe.transpose(ps6[:, N * r:N * r + N], ot[b.slot(2)][:, r, :], ident_s)
                        last.then_inc(S[ph, "ot_ps"], 1)
                    b = t + -3
                    if ph == CROSS and live(b):
                        pe.wait_ge(S[ph, "att_done"], b.count(1, 1))
                        need(pe, S[ph, "hid_done"], b.count(1))
                        pe.transpose(ps7[:, 0:N], att[b.slot(2)][:, :, :].rearrange("n h d -> n (h d)"),
                                     ident_s).then_inc(S[ph, "att_ps"], 1)
                    if live(t + -1):
                        weigh(t + -1, 0)
                    if live(t + 2):
                        scores(t + 2, 1, 0)
                        scores(t + 2, 1, 1)
                    if live(t):
                        shifted(t, 1, 0)
                        shifted(t, 1, 1)
                    b = t + -3
                    if ph == CROSS and live(b):
                        pe.wait_ge(S[ph, "att_sb"], b.count(1, 1))
                        pe.matmul(ps7[:, N:N + C], att_t[b.slot(2)][:, :], wt[:, O2, :], start=True,
                                  stop=True).then_inc(S[ph, "y_ps"], 1)
                    if live(t + -1):
                        weigh(t + -1, 1)

                for c in range(-2, B + 4):
                    step(Step(None, c))
                    if ph == SELF and c == B + 1:
                        turn(CROSS, Step(None, 0, 1))
                    if ph == CROSS and c > B:
                        front(c - B - 1)

            def front(g):
                if g >= 1:
                    pe.wait_ge(f_xsb, g)
                    for b in range(GB * (g - 1), GB * g):
                        last = pe.matmul(ps01[:, 1, E * b:E * b + E], xt_all[:, b, :], router_t[:, :], start=True, stop=True)
                    if g == NG:
                        last.then_inc(f_logits, 1)
                if g < NG:
                    pe.wait_ge(f_xh, g + 1)
                    if g == 0:
                        pe.wait_ge(S[CROSS, "max_done"], 4 * B)
                    if g >= 2:
                        pe.wait_ge(f_xsb, g - 1)
                    for j in range(GB):
                        last = pe.transpose((ps5[:, :], ps01[:, 0])[g % 2][:, N * j:N * j + N], (xh, xg)[g % 2][:, j, :],
                                            ident_s)
                    last.then_inc(f_xps, 1)

            turn(SELF, Step(None, 0, 1))
            groups(pe, project_self)
            for g in range(NG):
                if g < NG - 1:
                    turn(CONTEXT, Step(None, g + 1, 1))
                project(CONTEXT, g)
            attend(SELF)
            for g in range(NG):
                if 1 <= g < NG - 1:
                    turn(CROSS, Step(None, g + 1, 1))
                project(CROSS, g)
                if g == 0:
                    turn(CROSS, Step(None, 1, 1))
            attend(CROSS)
            for g in range(NG - 1, NG + 1):
                front(g)

            def expert(b):
                y = (ps23, ps01)[b.slot(2)]
                pe.wait_ge(f_xe, b.count(1, 1))
                if b.i is None and b.c == 1:
                    pe.wait_ge(f_link, 2)
                need(pe, f_acc, b.count(6, -6))
                need(pe, f_term, b.count(2, -2))
                for h, first in enumerate((0, 3, 6)):
                    bank = (y[:, 0], y[:, 1], (ps4, ps6)[b.slot(2)][:, :])[h]
                    count = (3, 3, 2)[h]
                    last = pe.matmul(bank[:, 0:count * C], xe[b.slot(2)][:, :],
                                     experts_s[:, first:first + count, :].rearrange("h e o -> h (e o)"), start=True, stop=True)
                last.then_inc(f_y, 1)

            pe.wait_ge(experts_in, 16)
            tiles(pe, expert)

        @block.scalar
        def _(act):
            act.dma_start(hid[:, 0:GB, :], x[0:GB].rearrange("b n c -> n b c")).then_inc(x_first, 16)
            act.dma_start(hid[:, GB:B, :], x[GB:B].rearrange("b n c -> n b c")).then_inc(x_in, 16)
            act.wait_ge(w_ps, 1)
            nc.scalar.copy(wt[:, 0:4, :].rearrange("i n o -> i (n o)"), ps01[:, 0])
            nc.scalar.copy(wt[:, 4, :], ps01[:, 1, 0:128]).then_inc(w_sb, 1)

            def copy_weights():
                act.wait_ge(w_ps, 2)
                nc.scalar.copy(wt[:, 5:9, :].rearrange("i n o -> i (n o)"), ps6[:, :])
                nc.scalar.copy(bqk[:, :], ps7[:, 0:2])
                nc.scalar.copy(router_t[:, :], ps7[:, 8:8 + E])
                nc.scalar.copy(bvo[:, :, :].rearrange("n a c -> n (a c)"), ps7[:, 128:384]).then_inc(w_sb, 1)
                act.wait_ge(w_sb, 2)

            def copy_inputs(ph, g):
                act.wait_ge(S[ph, "x_ps"], g.count(1, 1))
                need(act, S[ph, "proj"], g.count(3) if ph == SELF else
                     {CONTEXT: 2, CROSS: 1}[ph] * (g.c - 1))
                nc.scalar.copy(xts[0 if ph == SELF else g.c % 2][:, :], ps5[:, :]).then_inc(S[ph, "x_sb"], 1)

            def project_self(g, more):
                for o, whole in ((Q, "q_full"), (K, "k_full")):
                    act.wait_ge(S[SELF, whole], g.count(1, 1))
                    nc.scalar.copy(part_of(o, 0, g), full[o][:, :]).then_inc(S[SELF, "part1"], 1)
                    if o == Q:
                        act.wait_ge(S[SELF, "proj"], g.count(3, 3))
                        nc.scalar.copy(of_group(vall, g), batches(ps4[:, :])).then_inc(S[SELF, "v_sb"], 1)
                        if more:
                            copy_inputs(SELF, g + 1)
                        else:
                            copy_weights()
                            copy_inputs(CONTEXT, Step(None, 0, 1))
                for o in (Q, K):
                    act.wait_ge(S[SELF, "rest"], g.count(2, o + 1))
                    nc.scalar.copy(part_of(o, 1, g), rest[o][:, :]).then_inc(S[SELF, "part2"], 1)

            def project(ph, g):
                o = Q if ph == CROSS else CONTEXT_K
                if g < NG - 1 and not (ph == CROSS and g == 0):
                    copy_inputs(ph, Step(None, g + 1, 1))
                if g < NG:
                    act.wait_ge(S[ph, "full"], g + 1)
                    nc.scalar.copy(part_of(o, 0, Step(None, g, 1)), full[g % 2][:, :]).then_inc(S[ph, "part1"], 1)
                if ph == CROSS and g == 0:
                    copy_inputs(ph, Step(None, 1, 1))
                if g >= 1:
                    act.wait_ge(S[ph, "rest"], g)
                    nc.scalar.copy(part_of(o, 1, Step(None, g - 1, 1)), rest[(g - 1) % 2][:, :]).then_inc(S[ph, "part2"], 1)

            def attend(ph):
                def exponentials(b, u):
                    for a in range(2):
                        act.wait_ge(S[ph, "r_ps"], b.count(4, 2 * u + a + 1))
                        if u == 0:
                            need(act, S[ph, "pv"], b.count(1, -1))
                        nc.scalar.activation(probs[b.slot(2)][:, u, a, :, :].rearrange("m p n -> m (p n)"), ps23[:, a, :],
                                             ACT.Exp, scale=D ** -0.5).then_inc(S[ph, "exp_done"], 1)

                def step(t):
                    b = t + 1
                    if live(b):
                        act.wait_ge(S[ph, "shift_ps"], b.count(1, 1))
                        old = b + -2
                        if live(old):
                            act.wait_ge(shift_in[ph, old.slot(4)], old.turn(16, 16))
                        nc.scalar.copy(shift_t[b.slot(2)][:, :], ps5[0:4 * HALF, 0:N // 2].bitcast(BF16)).then_inc(
                            S[ph, "shift_sb"], 1)
                    if live(t):
                        exponentials(t, 0)
                    b = t + -3
                    if ph == CROSS and live(b):
                        act.wait_ge(S[ph, "att_ps"], b.count(1, 1))
                        need(act, S[ph, "y_ps"], b.count(1, -1))
                        nc.scalar.copy(att_t[b.slot(2)][:, :], ps7[:, 0:N]).then_inc(S[ph, "att_sb"], 1)
                    if live(t):
                        exponentials(t, 1)
                    b = t + -1
                    if live(b):
                        act.wait_ge(S[ph, "pv"], b.count(1, 1))
                        need(act, S[ph, "ot_ps"], b.count(1, -1))
                        nc.scalar.copy(ot[b.slot(2)][:, :, :].rearrange("c r n -> c (r n)"), ps4[:, 0:2 * N]).then_inc(
                            S[ph, "ot_sb"], 1)

                    if ph == SELF and t.i is None and t.c == B + 1:
                        copy_inputs(CROSS, Step(None, 0, 1))
                    if ph == CROSS and t.i is None and t.c > B:
                        front(t.c - B - 1)

                steps(act, step)

            def front(g):
                act.wait_ge(f_xps, g + 1)
                nc.scalar.copy(xt_all[:, GB * g:GB * (g + 1), :].rearrange("c b n -> c (b n)"),
                               (ps5[:, :], ps01[:, 0])[g % 2]).then_inc(f_xsb, 1)

            copy_inputs(SELF, Step(None, 0, 1))
            groups(act, project_self)
            for g in range(NG + 1):
                project(CONTEXT, g)
            attend(SELF)
            for g in range(NG + 1):
                project(CROSS, g)
            attend(CROSS)

            front(NG - 1)
            act.wait_ge(f_link, 2)
            nc.scalar.activation(g_p[:, :, :], g_l[:, :, :], ACT.Exp).then_inc(f_exp, 1)

            def copy_tile(b):
                need(act, f_y, b.count(1, -1))
                nc.scalar.copy(xe[b.slot(2)][:, :], xt_all[:, b.count(), :]).then_inc(f_xe, 1)

            def expert(b):
                if not (b.i is None and b.c >= B - 1):
                    copy_tile(b + 1)
                act.wait_ge(f_y, b.count(1, 1))
                if b.i is None and b.c == 0:
                    act.wait_ge(f_gate, 1)
                need(act, f_result, b.count(1, -1))
                for h in range(2):
                    nc.scalar.activation(term[b.slot(2)][h][:, :], (ps4, ps6)[b.slot(2)][:, C * h:C * h + C], ACT.Copy,
                                         scale=gate[:, b.count(), 6 + h:7 + h]).then_inc(f_term, 1)

            act.wait_ge(f_xsb, NG)
            copy_tile(Step(None, 0))
            tiles(act, expert)

        @block.vector
        def _(dve):
            nc.vector.memset(ones_row[:, :], 1.0).then_inc(dve_const, 1)
            nc.vector.memset(kst[:, 0, :, :, :], 0.0).then_inc(kst_zero, 1)

            def take_stats(first, end):
                for b in range(first, end):
                    nc.vector.bn_stats(stats[:, b, :], hid[:, b, :]).then_inc(x_stats, 1)

            def layernorm(done, k, first, end):
                ln, own, before = ln_step[k], slice(first, end), 7 if first else 0
                dve.wait_ge(done, end)
                nc.vector.tensor_tensor(ln_a[:, own], stats[:, own, 1], stats[:, own, 4], ALU.add).then_inc(ln, 1)
                nc.vector.tensor_tensor(ln_b[:, own], stats[:, own, 1], stats[:, own, 4], ALU.subtract).then_inc(ln, 1)
                nc.vector.tensor_tensor(ln_c[:, own], stats[:, own, 2], stats[:, own, 5], ALU.add).then_inc(ln, 1)
                dve.wait_ge(ln, before + 3)
                nc.vector.tensor_scalar(mean[:, own], ln_a[:, own], 0.5, None, ALU.mult).then_inc(ln, 1)
                nc.vector.scalar_tensor_tensor(ln_d[:, own], ln_b[:, own], 0.25, ln_b[:, own], ALU.mult, ALU.mult).then_inc(ln, 1)
                dve.wait_ge(ln, before + 5)
                nc.vector.scalar_tensor_tensor(ln_e[:, own], ln_c[:, own], 1.0 / C, ln_d[:, own], ALU.mult, ALU.add).then_inc(ln, 1)
                dve.wait_ge(ln, before + 6)
                nc.vector.tensor_scalar(ln_f[:, own], ln_e[:, own], EPS, None, ALU.add).then_inc(ln, 1)

            def normalise(g, k, last_read, done):
                dve.wait_ge(rstd_done[k], g.count(1, 1))
                need(dve, last_read, g.count(1))
                for j in range(GB):
                    b = g.count(GB, j)
                    last = nc.vector.tensor_scalar(xh[:, j, :], hid[:, b, :], mean[:, bass.ds(b, 1)], rstd[:, bass.ds(b, 1)],
                                                   ALU.subtract, ALU.mult)
                last.then_inc(done, 1)

            def inputs(ph, g):
                normalise(g, ph, S[ph, "x_ps"], S[ph, "xh_done"])

            def project(ph, g):
                if ph == CROSS and 1 <= g < NG - 1:
                    inputs(CROSS, Step(None, g + 1, 1))
                ps, n, per = (ps01, 0, 1) if ph == CROSS else (ps23, 1, 2)
                dve.wait_ge(S[ph, "proj"], per * g + 1)
                need(dve, S[ph, "rest"], g - 1)
                nc.vector.tensor_scalar(full[g % 2][:, :], ps[:, g % 2], bqk[:, n:n + 1], None, ALU.add).then_inc(
                    S[ph, "full"], 1)
                if ph == CROSS and g == 0:
                    inputs(CROSS, Step(None, 1, 1))
                if ph == CONTEXT:
                    dve.wait_ge(S[ph, "proj"], 2 * g + 2)
                    nc.vector.tensor_tensor(context[:, GB * g:GB * g + GB, :], batches((ps4, ps6)[g % 2][:, :]),
                                            bvo[:, 0:1, :].broadcast_to([128, GB, C]), ALU.add).then_inc(S[ph, "v_sb"], 1)

            def project_self(g, more):
                if more:
                    inputs(SELF, g + 1)
                cos_g = cos_s.unsqueeze(1).broadcast_to([128, GB, N])
                sin_g = sin_s.unsqueeze(1).broadcast_to([128, GB, N])
                for o, (ps, read, whole) in enumerate(((ps01, "q_read", "q_full"), (ps23, "k_read", "k_full"))):
                    dve.wait_ge(S[SELF, "proj"], g.count(3, o + 1))
                    need(dve, S[SELF, whole], g.count(1))
                    nc.vector.tensor_tensor(batches(rope_a[o][:, :]), batches(ps[:, 0]), cos_g, ALU.mult)
                    nc.vector.tensor_tensor(batches(rope_b[o][:, :]), batches(ps[:, 1]), sin_g, ALU.mult).then_inc(S[SELF, read], 1)
                    dve.wait_ge(S[SELF, read], g.count(1, 1))
                    need(dve, S[SELF, "rest"], g.count(2, o - 1))
                    nc.vector.tensor_tensor(full[o][:, :], rope_a[o][:, :], rope_b[o][:, :], ALU.add).then_inc(S[SELF, whole], 1)

            def attend(ph):
                def maxima(b, u):
                    if u == 0:
                        need(dve, S[ph, "shift_done"], b.count(1, -1))
                    for a in range(2):
                        dve.wait_ge(S[ph, "s_ps"], b.count(4, 2 * u + a + 1))
                        nc.vector.tensor_reduce(smax[b.slot(2)][:, a, 4 * u:4 * u + 4],
                                                ps01[:, a, :].rearrange("n (p m) -> n p m", p=4), AX.X,
                                                ALU.max).then_inc(S[ph, "max_done"], 1)

                def step(t):
                    if live(t + 2):
                        maxima(t + 2, 0)
                    b = t + -2
                    if live(b):
                        q = b.slot(2)
                        heads = ps6[:, 0:2 * N].rearrange("n (h e) -> n h e", h=H)
                        dve.wait_ge(S[ph, "ot_ps"], b.count(1, 1))
                        nc.vector.reciprocal(rsum[q][:, :].unsqueeze(2), heads[:, :, D:D + 1]).then_inc(S[ph, "rsum_done"], 1)
                        dve.wait_ge(S[ph, "rsum_done"], b.count(1, 1))
                        need(dve, S[ph, "hid_done" if ph == SELF else "att_ps"], b.count(1, -1))
                        nc.vector.tensor_tensor(att[q][:, :, :], heads[:, :, 0:D],
                                                rsum[q][:, :].unsqueeze(2).broadcast_to([128, H, D]),
                                                ALU.mult).then_inc(S[ph, "att_done"], 1)
                    if live(t + 2):
                        maxima(t + 2, 1)
                    b = t + -3
                    if ph == CROSS and live(b):
                        dve.wait_ge(S[ph, "y_ps"], b.count(1, 1))
                        dve.wait_ge(S[ph, "bias_done"], b.count(1, 1))
                        nc.vector.tensor_tensor(hid[:, b.count(), :], ps7[:, N:N + C], hid[:, b.count(), :],
                                                ALU.add).then_inc(S[ph, "hid_done"], 1)
                    b = t + (-3 if ph == SELF else -4)
                    if live(b):
                        dve.wait_ge(S[ph, "hid_done"], b.count(1, 1))
                        nc.vector.bn_stats(stats[:, b.count(), :], hid[:, b.count(), :]).then_inc(S[ph, "stat_done"], 1)

                    if t.i is None and t.c == B - 1:
                        layernorm(S[ph, "stat_done"], CROSS if ph == SELF else FFN, 0, B - GB)
                    if ph == SELF and t.i is None and t.c == B:
                        inputs(CROSS, Step(None, 0, 1))
                    if ph == CROSS and t.i is None and B <= t.c < B + NG - 1:
                        front(t.c - B)

                steps(dve, step)

            def front(g):
                dve.wait_ge(rstd_done[FFN], g + 1)
                if g >= 2:
                    dve.wait_ge(f_xps, g - 1)
                for j in range(GB):
                    b = GB * g + j
                    last = nc.vector.tensor_scalar((xh, xg)[g % 2][:, j, :], hid[:, b, :], mean[:, b:b + 1], rstd[:, b:b + 1],
                                                   ALU.subtract, ALU.mult)
                last.then_inc(f_xh, 1)

            dve.wait_ge(x_first, 16)
            take_stats(0, GB)
            layernorm(x_stats, SELF, 0, GB)
            dve.wait_ge(x_in, 16)
            take_stats(GB, 2 * GB)
            inputs(SELF, Step(None, 0, 1))
            take_stats(2 * GB, B)
            layernorm(x_stats, SELF, GB, B)
            dve.wait_ge(const_in, 16)
            nc.vector.tensor_copy(ident_b[:, :], ident_s).then_inc(dve_const, 1)
            nc.vector.memset(kst[:, 1, 0, :, :], 0.0).then_inc(kst_zero, 1)
            groups(dve, project_self)
            dve.wait_ge(S[SELF, "rest"], 2 * NG)
            for g in range(NG):
                project(CONTEXT, g)
            attend(SELF)
            layernorm(S[SELF, "stat_done"], CROSS, B - GB, B)
            for g in range(NG):
                project(CROSS, g)
            attend(CROSS)
            layernorm(S[CROSS, "stat_done"], FFN, B - GB, B)
            front(NG - 1)
            dve.wait_ge(pool_const, 3)

            def route():
                links = []

                def link(ins):
                    links.append(ins)
                    ins.then_inc(f_link, 1)
                    dve.wait_ge(f_link, len(links))

                def spread(k):
                    return g_s[:, k, :].unsqueeze(2).broadcast_to([128, B, E])

                logits = ps01[:, 1, 0:B * E].rearrange("n (b e) -> n b e", b=B)
                dve.wait_ge(f_logits, 1)
                link(nc.vector.tensor_reduce(g_s[:, 0, :], logits, AX.X, ALU.max))
                link(nc.vector.tensor_tensor(g_l[:, :, :], logits, spread(0), ALU.subtract))
                dve.wait_ge(f_exp, 1)
                link(nc.vector.tensor_reduce(g_s[:, 1, :], g_p[:, :, :], AX.X, ALU.add))
                link(nc.vector.reciprocal(g_s[:, 1, :], g_s[:, 1, :]))
                link(nc.vector.tensor_tensor(g_q[:, :, :], g_p[:, :, :], spread(1), ALU.mult))
                rest_q = g_q
                for k, first in enumerate(g_first):
                    link(nc.vector.tensor_reduce(g_s[:, 2 + k, :], rest_q[:, :, :], AX.X, ALU.max))
                    link(nc.vector.tensor_tensor(g_l[:, :, :], rest_q[:, :, :], spread(2 + k), ALU.is_equal))
                    link(nc.vector.tensor_tensor(g_l[:, :, :], g_l[:, :, :], falling[:, :].unsqueeze(1).broadcast_to([128, B, E]),
                                                 ALU.mult))
                    link(nc.vector.tensor_reduce(g_s[:, 4 + k, :], g_l[:, :, :], AX.X, ALU.max))
                    link(nc.vector.tensor_tensor(first[:, :, :], g_l[:, :, :], spread(4 + k), ALU.is_equal))
                    if k == 0:
                        rest_q = g_r
                        link(nc.vector.scalar_tensor_tensor(g_r[:, :, :], first[:, :, :], -2.0, g_q[:, :, :], ALU.mult, ALU.add))
                link(nc.vector.tensor_tensor(g_l[:, :, :], g_first[0][:, :, :], g_first[1][:, :, :], ALU.add))
                link(nc.vector.tensor_tensor(g_w[:, :, :], g_l[:, :, :], g_q[:, :, :], ALU.mult))
                link(nc.vector.tensor_reduce(g_s[:, 6, :], g_w[:, :, :], AX.X, ALU.add))
                link(nc.vector.tensor_scalar(g_s[:, 6, :], g_s[:, 6, :], 1e-6, None, ALU.add))
                link(nc.vector.reciprocal(g_s[:, 6, :], g_s[:, 6, :]))
                link(nc.vector.tensor_tensor(gate[:, :, :], g_w[:, :, :], spread(6), ALU.mult))
                link(nc.vector.tensor_tensor(g_r[:, :, :], gate[:, :, :], g_q[:, :, :], ALU.mult))
                nc.vector.tensor_reduce(gbias[:, :], g_r[:, :, :], AX.X, ALU.add).then_inc(f_gate, 1)

            def expert(b):
                q, k = b.slot(2), b.count()
                dve.wait_ge(f_y, b.count(1, 1))
                if b.c == 0 and b.i is None:
                    dve.wait_ge(f_gate, 1)
                need(dve, f_result, b.count(1, -1))
                for e in range(3):
                    for h in range(2):
                        y = (ps23, ps01)[q][:, h, C * e:C * e + C]
                        w = gate[:, k, 3 * h + e:3 * h + e + 1]
                        total = acc[q][h]
                        if e:
                            dve.wait_ge(f_acc, b.count(6, 2 * e + h - 1))
                            ins = nc.vector.scalar_tensor_tensor(total[:, :], y, w, total[:, :], ALU.mult, ALU.add)
                        elif h == 0:
                            ins = nc.vector.scalar_tensor_tensor(total[:, :], y, w, hid[:, k, :], ALU.mult, ALU.add)
                        else:
                            ins = nc.vector.tensor_scalar(total[:, :], y, w, gbias[:, bass.ds(k, 1)], ALU.mult, ALU.add)
                        ins.then_inc(f_acc, 1)

            route()
            tiles(dve, expert)

        @block.gpsimd
        def _(pool):
            nc.gpsimd.memset(minus_half[:, :], -0.5)
            nc.gpsimd.memset(minus_ones[:, :], -1.0).then_inc(pool_const, 1)
            pool.wait_ge(pool_const, 1)

            def root(k, *of):
                for g in of:
                    own = slice(GB * g, GB * (g + 1))
                    pool.wait_ge(ln_step[k], 14 if g >= (1 if k == SELF else NG - 1) else 7)
                    nc.gpsimd.tensor_tensor(rstd[:, own], ln_f[:, own], minus_half[:, own], ALU.pow).then_inc(rstd_done[k], 1)

            def project_self(g, more):
                for o in (Q, K):
                    pool.wait_ge(S[SELF, "part1"], g.count(2, o + 1))
                    need(pool, S[SELF, "part2"], g.count(2, o - 1))
                    need(pool, S[SELF, "part3"], g.count(2, o - 1))
                    nc.gpsimd.tensor_tensor(rest[o][:, :], full[o][:, :], part_of(o, 0, g), ALU.subtract).then_inc(
                        S[SELF, "rest"], 1)
                for o in (Q, K):
                    pool.wait_ge(S[SELF, "part2"], g.count(2, o + 1))
                    pool.wait_ge(S[SELF, "rest"], g.count(2, o + 1))
                    nc.gpsimd.tensor_tensor(part_of(o, 2, g), rest[o][:, :], part_of(o, 1, g), ALU.subtract).then_inc(
                        S[SELF, "part3"], 1)

            def project(ph, g):
                o = Q if ph == CROSS else CONTEXT_K
                if g < NG:
                    pool.wait_ge(S[ph, "part1"], g + 1)
                    need(pool, S[ph, "part2"], g - 1)
                    need(pool, S[ph, "part3"], g - 1)
                    nc.gpsimd.tensor_tensor(rest[g % 2][:, :], full[g % 2][:, :], part_of(o, 0, Step(None, g, 1)),
                                            ALU.subtract).then_inc(S[ph, "rest"], 1)
                if g >= 1:
                    last = Step(None, g - 1, 1)
                    pool.wait_ge(S[ph, "part2"], g)
                    nc.gpsimd.tensor_tensor(part_of(o, 2, last), rest[last.c % 2][:, :], part_of(o, 1, last),
                                            ALU.subtract).then_inc(S[ph, "part3"], 1)

            def attend(ph):
                pool.wait_ge(S[SELF if ph == SELF else CONTEXT, "v_sb"], NG)
                pool.wait_ge(S[ph, "xh_done"], NG)

                def step(t):
                    b = t
                    if live(b):
                        need(pool, S[ph, "pv"], b.count(1, -1))
                        values = (vall if ph == SELF else context)[:, b.count(), :].rearrange("m (j s d) -> m j s d", s=2, d=D)
                        for s in range(2):
                            last = nc.gpsimd.tensor_tensor(vpad[b.slot(2)][:, :, s, 2 * D * s:2 * D * s + D], values[:, :, s, :],
                                                           zeros[:, :].rearrange("n (j d) -> n j d", j=HALF), ALU.add)
                        last.then_inc(S[ph, "vpad_done"], 1)
                    b = t + -2
                    if live(b):
                        row = hid[:, b.count(), :]
                        if ph == SELF:
                            pool.wait_ge(S[ph, "att_done"], b.count(1, 1))
                            nc.gpsimd.tensor_tensor(row, att[b.slot(2)][:, :, :].rearrange("n h d -> n (h d)"), row,
                                                    ALU.add).then_inc(S[ph, "hid_done"], 1)
                        else:
                            nc.gpsimd.tensor_tensor(row, bvo[:, 1, :], row, ALU.add).then_inc(S[ph, "bias_done"], 1)
                    b = t + 2
                    if live(b):
                        q = b.slot(2)
                        pool.wait_ge(S[ph, "max_done"], b.count(4, 4))
                        need(pool, S[ph, "shift_ps"], b.count(1, -1))
                        nc.gpsimd.tensor_tensor(shift[q][:, :, 0, :], smax[q][:, :, :],
                                                zeros[:, 0:H].rearrange("n (a p) -> n a p", a=2), ALU.add).then_inc(S[ph, "shift_hi"], 1)
                        pool.wait_ge(S[ph, "shift_hi"], b.count(1, 1))
                        nc.gpsimd.tensor_tensor(shift[q][:, :, 1, :], smax[q][:, :, :], shift[q][:, :, 0, :],
                                                ALU.subtract).then_inc(S[ph, "shift_done"], 1)

                    if ph == SELF and t.i is None and t.c == B - 1:
                        root(CROSS, 0)
                    if ph == CROSS and t.i is None and B - 1 <= t.c < B + NG - 2:
                        root(FFN, t.c - B + 1)

                steps(pool, step)

            def constants():
                nc.gpsimd.memset(kst[:, 1, 1, :, :], 0.0).then_inc(kst_zero, 1)
                nc.gpsimd.memset(zeros[:, :], 0.0)
                for q in range(2):
                    nc.gpsimd.memset(vpad[q][:, :, :, :], 0.0)
                for e in range(E):
                    last = nc.gpsimd.memset(falling[:, e:e + 1], float(E - e))
                last.then_inc(pool_const, 1)
                pool.wait_ge(pool_const, 2)
                for q in range(2):
                    for s in range(2):
                        last = nc.gpsimd.memset(vpad[q][:, :, s, 2 * D * s + D:2 * D * s + 2 * D], 1.0)
                last.then_inc(pool_const, 1)
                pool.wait_ge(pool_const, 3)

            root(SELF, *range(NG))
            constants()
            groups(pool, project_self)
            for part_sem in ("part2", "part3"):
                pool.wait_ge(S[SELF, part_sem], 2 * NG)
            for g in range(NG + 1):
                project(CONTEXT, g)
            attend(SELF)
            root(CROSS, *range(1, NG))
            for g in range(NG + 1):
                project(CROSS, g)
            attend(CROSS)
            root(FFN, NG - 1)

            def expert(b):
                (s0, s1), (t0, t1), q = acc[b.slot(2)], term[b.slot(2)], b.slot(2)
                pool.wait_ge(f_term, b.count(2, 2))
                need(pool, f_result, b.count(1, -1))
                nc.gpsimd.tensor_tensor(terms[q][:, :], t0[:, :], t1[:, :], ALU.add).then_inc(f_terms, 1)
                pool.wait_ge(f_acc, b.count(6, 6))
                nc.gpsimd.tensor_tensor(sums[q][:, :], s0[:, :], s1[:, :], ALU.add).then_inc(f_sums, 1)
                pool.wait_ge(f_terms, b.count(1, 1))
                pool.wait_ge(f_sums, b.count(1, 1))
                nc.gpsimd.tensor_tensor(hid[:, b.count(), :], terms[q][:, :], sums[q][:, :], ALU.add).then_inc(f_result, 1)

            tiles(pool, expert)


NAMES = ["x", "ctx_1024", "L0_attn_Wq", "L0_attn_Wk", "L0_attn_Wv", "L0_xattn_Wq", "L0_xattn_bq", "L0_xattn_Wk",
         "L0_xattn_bk", "L0_xattn_Wv", "L0_xattn_bv", "L0_xattn_Wo", "L0_xattn_bo", "L0_ffn_router_w",
         "L0_ffn_expert_weights"]


def shape_constants():
    ident = np.eye(C, dtype=np.float32)
    order, rotate = np.zeros((C, C), np.float32), np.zeros((C, C), np.float32)
    cosines, sines = np.zeros((C, N), np.float32), np.zeros((C, N), np.float32)
    inv = np.power(np.float32(10000.0), (np.float32(-2.0) * np.arange(D // 2, dtype=np.float32) / np.float32(D)), dtype=np.float32)
    angle = np.arange(N, dtype=np.float32)[:, None] * inv[None, :]
    for a in range(2):
        for d in range(D):
            for p in range(HALF):
                row = (d * 2 + a) * HALF + p
                channel = (a * HALF + p) * D + d
                order[channel, row] = 1.0
                if d % 2 == 0:
                    rotate[channel + 1, row] = -1.0
                else:
                    rotate[channel - 1, row] = 1.0
                cosines[row], sines[row] = np.cos(angle[:, d // 2]), np.sin(angle[:, d // 2])
    return {"constants": np.stack([ident, order, rotate, cosines, sines])}


def kernel(**inputs):
    import concourse.bacc as bacc
    from concourse.bass_utils import run_bass_kernel_spmd as run

    nc = bacc.Bacc("TRN2", target_bir_lowering=False, num_devices=1)
    arrays, args = {}, []
    for name, a in [(n, np.ascontiguousarray(inputs[n])) for n in NAMES] + list(shape_constants().items()):
        arrays[f"in_{name}"] = a
        args.append(nc.dram_tensor(f"in_{name}", a.shape, mybir.dt.from_np(a.dtype), kind="ExternalInput").ap())
    args.append(nc.dram_tensor("out", (B, N, C), F32, kind="ExternalOutput").ap())
    build(nc, *args)
    r = run(nc, [arrays], core_ids=[0])
    return r.results[0]["out"]
```
